# Optimizing a Trainium2 kernel written in Bass

```python
import numpy as np
import jax
import jax.numpy as jnp

def _softmax(x, axis=-1):
    return jax.nn.softmax(x, axis=axis)

def _gelu(x):
    return jax.nn.gelu(x, approximate=True)

def _silu(x):
    return jax.nn.silu(x)

def _sigmoid(x):
    return jax.nn.sigmoid(x)

def _layernorm(x, axis=-1, eps=1e-05):
    m = jnp.mean(x, axis=axis, keepdims=True)
    v = jnp.var(x, axis=axis, keepdims=True)
    return (x - m) / jnp.sqrt(v + eps)

def _scatter_add(tgt, idx, src, axis=0):
    return tgt.at[idx].add(src)

def _segment_sum(src, seg, n):
    return jax.ops.segment_sum(src, seg, n)
kernel_name = 'mk_flamingo_gated_d1_seqx_r4_5340b7'

def setup_inputs(seed: int=0):
    np.random.seed(seed)
    _w = jnp.asarray

    def _rec_inputs():
        import jax
        import jax.numpy as jnp
        _rk = jax.random.key(seed)
        x = -0.0005207 + 1.001 * jax.random.normal(jax.random.fold_in(_rk, 1), (4, 512, 256), jnp.float32)
        _lenS = 512 - jax.random.randint(jax.random.fold_in(_rk, 7), (4,), 0, max(1, 512 // 4) + 1, jnp.int32)
        _lenS2 = 64 - jax.random.randint(jax.random.fold_in(_rk, 8), (4,), 0, max(1, 64 // 4) + 1, jnp.int32)
        _ctx_1024P = jax.random.normal(jax.random.fold_in(_rk, 11), (4, 16, 256), jnp.float32)
        _ctx_1024c = jax.random.dirichlet(jax.random.fold_in(_rk, 511), 0.3 * jnp.ones((16,), jnp.float32), (4, 64))
        _ctx_1024t = jnp.einsum('bsk,bkd->bsd', _ctx_1024c, _ctx_1024P)
        _ctx_1024t = _ctx_1024t * jax.lax.rsqrt(jnp.mean(jnp.square(_ctx_1024t)) + 1e-12) * 0.953939
        ctx_1024 = -0.000514642 + 1.00011 * (_ctx_1024t + 0.3 * jax.random.normal(jax.random.fold_in(_rk, 611), (4, 64, 256), jnp.float32))
        _g = jax.random.normal(jax.random.fold_in(_rk, 9001), (2, 1), jnp.float32)
        _g = jnp.sign(_g) * jnp.maximum(jnp.abs(_g), 1.0) + (_g == 0) * 1.0
        g_xattn = _g[0]
        g_ffn = _g[1]
        return (x, ctx_1024, g_xattn, g_ffn)
    x, ctx_1024, g_xattn, g_ffn = _rec_inputs()

    def _L0_xattn_setup():
        import jax, jax.numpy as jnp
        import numpy as np
        import math
        B, S, D, H = (1, 512, 256, 16)
        DK = D // H
        DH = 64
        LOG_T_MIN = math.log(0.1)
        LOG_T_MAX = math.log(10.0)

        def _linear(x, W, b):
            return x @ W.T + b
        key = jax.random.key(seed)
        ks = jax.random.split(key, 20)
        p = 0.02
        return {'query': jax.random.normal(ks[0], (B, S, D), jnp.float32), 'key': jax.random.normal(ks[1], (B, S, D), jnp.float32), 'value': jax.random.normal(ks[2], (B, S, D), jnp.float32), 'Wq': jax.random.normal(ks[3], (D, D), jnp.float32) * p, 'bq': jax.random.normal(ks[4], (D,), jnp.float32) * p, 'Wk': jax.random.normal(ks[5], (D, D), jnp.float32) * p, 'bk': jax.random.normal(ks[6], (D,), jnp.float32) * p, 'Wv': jax.random.normal(ks[7], (D, D), jnp.float32) * p, 'bv': jax.random.normal(ks[8], (D,), jnp.float32) * p, 'Wo': jax.random.normal(ks[9], (D, D), jnp.float32) * p, 'bo': jax.random.normal(ks[10], (D,), jnp.float32) * p, 'w1': jax.random.normal(ks[11], (DH, 3), jnp.float32) * 0.3, 'b1': jax.random.normal(ks[12], (DH,), jnp.float32) * 0.1, 'w2': jax.random.normal(ks[13], (DH, DH), jnp.float32) * 0.1, 'b2': jax.random.normal(ks[14], (DH,), jnp.float32) * 0.1, 'w3': jax.random.normal(ks[15], (1, DH), jnp.float32) * 0.1, 'b3': jnp.full((1,), (LOG_T_MIN + LOG_T_MAX) / 2, jnp.float32)}
    _L0_xattn_all = _L0_xattn_setup()
    _L0_xattn_in = {k: v for k, v in _L0_xattn_all.items() if k in ('Wq', 'bq', 'Wk', 'bk', 'Wv', 'bv', 'Wo', 'bo', 'w1', 'b1', 'w2', 'b2', 'w3', 'b3')}
    del _L0_xattn_all

    def _L0_ffn_setup():
        import jax, jax.numpy as jnp
        import numpy as np
        DIM = 256
        DEPTH = 6
        HEADS = 16
        DIM_HEAD = 64
        WINDOW = 64
        INNER = HEADS * DIM_HEAD
        DIM_INNER = int(DIM * 4 * 2 / 3)
        QK_SCALE = 8.0

        def shift_tokens(t):
            a, s = jnp.split(t, 2, -1)
            s = jnp.pad(s, ((0, 0), (1, 0), (0, 0)))[:, :-1]
            return jnp.concatenate([a, s], -1)

        def l2norm(t):
            return t / jnp.maximum(jnp.linalg.norm(t, axis=-1, keepdims=True), 1e-12)

        def rotate_half(x):
            x1, x2 = jnp.split(x, 2, -1)
            return jnp.concatenate([-x2, x1], -1)

        def rotary_tables(n):
            half = jnp.arange(0, DIM_HEAD, 2, dtype=jnp.float32)
            inv_freq = 1.0 / 10000.0 ** (half / DIM_HEAD)
            t = jnp.arange(n, dtype=jnp.float32)
            freqs = t[:, None] * inv_freq[None, :]
            freqs = jnp.concatenate([freqs, freqs], -1)
            base_scale = (half + 0.4 * DIM_HEAD) / (1.4 * DIM_HEAD)
            power = (t - n // 2) / (WINDOW // 2)
            scale = base_scale[None, :] ** power[:, None]
            scale = jnp.concatenate([scale, scale], -1)
            return (freqs, scale)

        def local_attention(q, k, v):
            b, h, n, d = q.shape
            w = WINDOW
            nw = n // w
            bq = q.reshape(b, h, nw, w, d)
            bk = k.reshape(b, h, nw, w, d)
            bv = v.reshape(b, h, nw, w, d)

            def look(t):
                p = jnp.pad(t, ((0, 0), (0, 0), (1, 0), (0, 0), (0, 0)))
                return jnp.concatenate([p[:, :, :nw], p[:, :, 1:]], axis=3)
            bk2, bv2 = (look(bk), look(bv))
            seq = jnp.arange(n).reshape(nw, w)
            seq_p = jnp.pad(seq, ((1, 0), (0, 0)), constant_values=-1)
            jt = jnp.concatenate([seq_p[:nw], seq_p[1:]], axis=1)
            it = seq[:, :, None]
            jb = jt[:, None, :]
            mask = (it < jb) | (it > jb + w) | (jb == -1)
            sim = jnp.einsum('bhwie,bhwje->bhwij', bq, bk2) * QK_SCALE
            sim = jnp.where(mask, -jnp.finfo(sim.dtype).max, sim)
            attn = jax.nn.softmax(sim, -1)
            out = jnp.einsum('bhwij,bhwje->bhwie', attn, bv2)
            return out.reshape(b, h, n, d)

        def attn_layer(x, Wqkv, qs, ksc, Wo):
            b, n, _ = x.shape
            qkv = x @ Wqkv
            q, k, v = jnp.split(qkv, 3, -1)
            sh = lambda t: t.reshape(b, n, HEADS, DIM_HEAD).transpose(0, 2, 1, 3)
            q, k, v = (sh(q), sh(k), sh(v))
            q = l2norm(q) * qs
            k = l2norm(k) * ksc
            freqs, scale = rotary_tables(n)
            cos, sin = (jnp.cos(freqs), jnp.sin(freqs))
            q = q * cos * scale + rotate_half(q) * sin * scale
            inv = 1.0 / scale
            k = k * cos * inv + rotate_half(k) * sin * inv
            out = local_attention(q, k, v)
            out = out.transpose(0, 2, 1, 3).reshape(b, n, INNER)
            return out @ Wo

        def ffn_layer(x, g, bln, W1, b1, W2, b2):
            mu = x.mean(-1, keepdims=True)
            var = ((x - mu) ** 2).mean(-1, keepdims=True)
            xn = (x - mu) / jnp.sqrt(var + 1e-05) * g + bln
            hg = xn @ W1 + b1
            a, gate = jnp.split(hg, 2, -1)
            return a * jax.nn.gelu(gate, approximate=False) @ W2 + b2
        key = jax.random.key(seed)
        ks = jax.random.split(key, 8)
        B, N = (2, 512)
        init = lambda k, shape: jax.random.normal(k, shape, jnp.float32) * 0.02
        return {'x': jax.random.normal(ks[0], (B, N, DIM), jnp.float32), 'Wqkv': init(ks[1], (DEPTH, DIM, 3 * INNER)), 'q_scale': jnp.ones((DEPTH, DIM_HEAD), jnp.float32), 'k_scale': jnp.ones((DEPTH, DIM_HEAD), jnp.float32), 'Wo': init(ks[2], (DEPTH, INNER, DIM)), 'ln_g': jnp.ones((DEPTH, DIM), jnp.float32), 'ln_b': jnp.zeros((DEPTH, DIM), jnp.float32), 'W1': init(ks[3], (DEPTH, DIM, 2 * DIM_INNER)), 'b1': jnp.zeros((DEPTH, 2 * DIM_INNER), jnp.float32), 'W2': init(ks[4], (DEPTH, DIM_INNER, DIM)), 'b2': jnp.zeros((DEPTH, DIM), jnp.float32)}
    _L0_ffn_all = _L0_ffn_setup()
    _L0_ffn_in = {k: v for k, v in _L0_ffn_all.items() if k in ('Wqkv', 'q_scale', 'k_scale', 'Wo', 'ln_g', 'ln_b', 'W1', 'b1', 'W2', 'b2')}
    del _L0_ffn_all
    return {'x': x, 'ctx_1024': ctx_1024, 'g_xattn': g_xattn, 'g_ffn': g_ffn, 'L0_xattn_Wq': _L0_xattn_in['Wq'], 'L0_xattn_bq': _L0_xattn_in['bq'], 'L0_xattn_Wk': _L0_xattn_in['Wk'], 'L0_xattn_bk': _L0_xattn_in['bk'], 'L0_xattn_Wv': _L0_xattn_in['Wv'], 'L0_xattn_bv': _L0_xattn_in['bv'], 'L0_xattn_Wo': _L0_xattn_in['Wo'], 'L0_xattn_bo': _L0_xattn_in['bo'], 'L0_xattn_w1': _L0_xattn_in['w1'], 'L0_xattn_b1': _L0_xattn_in['b1'], 'L0_xattn_w2': _L0_xattn_in['w2'], 'L0_xattn_b2': _L0_xattn_in['b2'], 'L0_xattn_w3': _L0_xattn_in['w3'], 'L0_xattn_b3': _L0_xattn_in['b3'], 'L0_ffn_Wqkv': _L0_ffn_in['Wqkv'], 'L0_ffn_q_scale': _L0_ffn_in['q_scale'], 'L0_ffn_k_scale': _L0_ffn_in['k_scale'], 'L0_ffn_Wo': _L0_ffn_in['Wo'], 'L0_ffn_ln_g': _L0_ffn_in['ln_g'], 'L0_ffn_ln_b': _L0_ffn_in['ln_b'], 'L0_ffn_W1': _L0_ffn_in['W1'], 'L0_ffn_b1': _L0_ffn_in['b1'], 'L0_ffn_W2': _L0_ffn_in['W2'], 'L0_ffn_b2': _L0_ffn_in['b2']}

def reference(x, ctx_1024, g_xattn, g_ffn, L0_xattn_Wq, L0_xattn_bq, L0_xattn_Wk, L0_xattn_bk, L0_xattn_Wv, L0_xattn_bv, L0_xattn_Wo, L0_xattn_bo, L0_xattn_w1, L0_xattn_b1, L0_xattn_w2, L0_xattn_b2, L0_xattn_w3, L0_xattn_b3, L0_ffn_Wqkv, L0_ffn_q_scale, L0_ffn_k_scale, L0_ffn_Wo, L0_ffn_ln_g, L0_ffn_ln_b, L0_ffn_W1, L0_ffn_b1, L0_ffn_W2, L0_ffn_b2):
    import jax
    import jax.numpy as jnp

    def _L0_xattn_ref(query, key, value, Wq, bq, Wk, bk, Wv, bv, Wo, bo, w1, b1, w2, b2, w3, b3):
        import jax, jax.numpy as jnp
        import numpy as np
        import math
        B, S, D, H = (1, 512, 256, 16)
        DK = D // H
        DH = 64
        LOG_T_MIN = math.log(0.1)
        LOG_T_MAX = math.log(10.0)

        def _linear(x, W, b):
            return x @ W.T + b
        b, sq, d = query.shape
        sk = key.shape[1]
        h, dk = (H, DK)
        Q = _linear(query, Wq, bq).reshape(b, sq, h, dk).transpose(0, 2, 1, 3)
        K = _linear(key, Wk, bk).reshape(b, sk, h, dk).transpose(0, 2, 1, 3)
        V = _linear(value, Wv, bv).reshape(b, sk, h, dk).transpose(0, 2, 1, 3)
        qk = jnp.einsum('bhqd,bhkd->bhqk', Q, K)
        scores = qk / math.sqrt(dk)
        mean_sim = scores.mean(axis=(-2, -1))
        max_sim = scores.max(axis=-1).mean(axis=-1)
        probs = jax.nn.softmax(scores, axis=-1)
        entropy_proxy = jnp.var(probs, axis=-1, ddof=1).mean(axis=-1)
        feats = jnp.stack([mean_sim, max_sim, entropy_proxy], axis=-1)
        hidden = jax.nn.gelu(_linear(feats, w1, b1), approximate=False)
        hidden = jax.nn.gelu(_linear(hidden, w2, b2), approximate=False)
        log_t = jnp.clip(_linear(hidden, w3, b3), LOG_T_MIN, LOG_T_MAX)
        t = jnp.exp(log_t)[..., None]
        attn_scores = qk / (2.0 * t)
        attn = jax.nn.softmax(attn_scores, axis=-1)
        attn = jnp.nan_to_num(attn, nan=0.0)
        out = jnp.einsum('bhqk,bhkd->bhqd', attn, V)
        out = out.transpose(0, 2, 1, 3).reshape(b, sq, d)
        return _linear(out, Wo, bo)

    def _L0_ffn_ref(x, Wqkv, q_scale, k_scale, Wo, ln_g, ln_b, W1, b1, W2, b2):
        import jax, jax.numpy as jnp
        import numpy as np
        DIM = 256
        DEPTH = 6
        HEADS = 16
        DIM_HEAD = 64
        WINDOW = 64
        INNER = HEADS * DIM_HEAD
        DIM_INNER = int(DIM * 4 * 2 / 3)
        QK_SCALE = 8.0

        def shift_tokens(t):
            a, s = jnp.split(t, 2, -1)
            s = jnp.pad(s, ((0, 0), (1, 0), (0, 0)))[:, :-1]
            return jnp.concatenate([a, s], -1)

        def l2norm(t):
            return t / jnp.maximum(jnp.linalg.norm(t, axis=-1, keepdims=True), 1e-12)

        def rotate_half(x):
            x1, x2 = jnp.split(x, 2, -1)
            return jnp.concatenate([-x2, x1], -1)

        def rotary_tables(n):
            half = jnp.arange(0, DIM_HEAD, 2, dtype=jnp.float32)
            inv_freq = 1.0 / 10000.0 ** (half / DIM_HEAD)
            t = jnp.arange(n, dtype=jnp.float32)
            freqs = t[:, None] * inv_freq[None, :]
            freqs = jnp.concatenate([freqs, freqs], -1)
            base_scale = (half + 0.4 * DIM_HEAD) / (1.4 * DIM_HEAD)
            power = (t - n // 2) / (WINDOW // 2)
            scale = base_scale[None, :] ** power[:, None]
            scale = jnp.concatenate([scale, scale], -1)
            return (freqs, scale)

        def local_attention(q, k, v):
            b, h, n, d = q.shape
            w = WINDOW
            nw = n // w
            bq = q.reshape(b, h, nw, w, d)
            bk = k.reshape(b, h, nw, w, d)
            bv = v.reshape(b, h, nw, w, d)

            def look(t):
                p = jnp.pad(t, ((0, 0), (0, 0), (1, 0), (0, 0), (0, 0)))
                return jnp.concatenate([p[:, :, :nw], p[:, :, 1:]], axis=3)
            bk2, bv2 = (look(bk), look(bv))
            seq = jnp.arange(n).reshape(nw, w)
            seq_p = jnp.pad(seq, ((1, 0), (0, 0)), constant_values=-1)
            jt = jnp.concatenate([seq_p[:nw], seq_p[1:]], axis=1)
            it = seq[:, :, None]
            jb = jt[:, None, :]
            mask = (it < jb) | (it > jb + w) | (jb == -1)
            sim = jnp.einsum('bhwie,bhwje->bhwij', bq, bk2) * QK_SCALE
            sim = jnp.where(mask, -jnp.finfo(sim.dtype).max, sim)
            attn = jax.nn.softmax(sim, -1)
            out = jnp.einsum('bhwij,bhwje->bhwie', attn, bv2)
            return out.reshape(b, h, n, d)

        def attn_layer(x, Wqkv, qs, ksc, Wo):
            b, n, _ = x.shape
            qkv = x @ Wqkv
            q, k, v = jnp.split(qkv, 3, -1)
            sh = lambda t: t.reshape(b, n, HEADS, DIM_HEAD).transpose(0, 2, 1, 3)
            q, k, v = (sh(q), sh(k), sh(v))
            q = l2norm(q) * qs
            k = l2norm(k) * ksc
            freqs, scale = rotary_tables(n)
            cos, sin = (jnp.cos(freqs), jnp.sin(freqs))
            q = q * cos * scale + rotate_half(q) * sin * scale
            inv = 1.0 / scale
            k = k * cos * inv + rotate_half(k) * sin * inv
            out = local_attention(q, k, v)
            out = out.transpose(0, 2, 1, 3).reshape(b, n, INNER)
            return out @ Wo

        def ffn_layer(x, g, bln, W1, b1, W2, b2):
            mu = x.mean(-1, keepdims=True)
            var = ((x - mu) ** 2).mean(-1, keepdims=True)
            xn = (x - mu) / jnp.sqrt(var + 1e-05) * g + bln
            hg = xn @ W1 + b1
            a, gate = jnp.split(hg, 2, -1)
            return a * jax.nn.gelu(gate, approximate=False) @ W2 + b2
        for i in range(DEPTH):
            x = attn_layer(shift_tokens(x), Wqkv[i], q_scale[i], k_scale[i], Wo[i]) + x
            x = ffn_layer(shift_tokens(x), ln_g[i], ln_b[i], W1[i], b1[i], W2[i], b2[i]) + x
        return x
    x = x + jnp.tanh(g_xattn[0]) * _L0_xattn_ref(_layernorm(x, axis=-1), ctx_1024, ctx_1024, L0_xattn_Wq, L0_xattn_bq, L0_xattn_Wk, L0_xattn_bk, L0_xattn_Wv, L0_xattn_bv, L0_xattn_Wo, L0_xattn_bo, L0_xattn_w1, L0_xattn_b1, L0_xattn_w2, L0_xattn_b2, L0_xattn_w3, L0_xattn_b3)
    x = x + jnp.tanh(g_ffn[0]) * _L0_ffn_ref(_layernorm(x, axis=-1), L0_ffn_Wqkv, L0_ffn_q_scale, L0_ffn_k_scale, L0_ffn_Wo, L0_ffn_ln_g, L0_ffn_ln_b, L0_ffn_W1, L0_ffn_b1, L0_ffn_W2, L0_ffn_b2)
    return x

_drawn_inputs = setup_inputs


def setup_inputs(seed=0):
    import zlib

    import numpy as np

    out = dict(_drawn_inputs(seed))
    spreads = {'L0_ffn_q_scale': (1.0, 0.2),
     'L0_ffn_k_scale': (1.0, 0.2),
     'L0_ffn_ln_g': (1.0, 0.2),
     'L0_ffn_ln_b': (0.0, 0.1),
     'L0_ffn_b1': (0.0, 0.1),
     'L0_ffn_b2': (0.0, 0.1)}
    factors = {'L0_xattn_Wq': 8.0,
     'L0_xattn_bq': 8.0,
     'L0_xattn_Wk': 8.0,
     'L0_xattn_bk': 8.0,
     'L0_xattn_bv': 6.271,
     'L0_xattn_w1': 8.0,
     'L0_xattn_b1': 8.0,
     'L0_xattn_w2': 8.0,
     'L0_xattn_b2': 8.0,
     'L0_xattn_w3': 8.0}
    for name, (base, spread) in spreads.items():
        noise = np.random.default_rng([zlib.crc32(name.encode()), seed]).standard_normal(out[name].shape)
        drawn = base * np.exp(spread * noise) if base else spread * noise
        out[name] = jnp.asarray(drawn.astype(out[name].dtype))
    for name, factor in factors.items():
        out[name] = (out[name] * factor).astype(out[name].dtype)
    return out
```

```python
from contextlib import ExitStack

import numpy as np

import concourse.bass as bass
from concourse import mybir

F32 = mybir.dt.float32
F32R = mybir.dt.float32r
BF16 = mybir.dt.bfloat16
I32 = mybir.dt.int32
ALU = mybir.AluOpType
ACT = mybir.ActivationFunctionType
AX = mybir.AxisListType

P = 128
B, S, D = 4, 512, 256
CTX = 64
XH, XD = 16, 16
KC = D // P
TILES = S // P
DEPTH, H, DH, W = 6, 16, 64, 64
INNER = H * DH
PAIRS = H // 2
HID = int(D * 4 * 2 / 3)
HC = -(-HID // P)
LAST = HID - (HC - 1) * P
ROW = S + 1
ITERS = DEPTH * B
COLUMN = (0, INNER, 512, INNER + 512, 2 * INNER, 2 * INNER + 512)
CHUNKS = len(COLUMN)
MASKED = -1.0e30
FFN_LOADS = 6
MAGIC = float(0x5F3759DF)
NEWTON = 3


class Signal:

    def __init__(self, sem, per, credit=0):
        self.sem, self.per, self.credit = sem, per, credit

    def at(self, unit, n):
        value = unit * self.per + (n + self.credit)
        assert not isinstance(value, int) or value > 0
        return value


class Buffers:
    pass


def bcast(ap, shape):
    return ap.to_broadcast(list(shape))


def build(nc, a):
    with ExitStack() as ctx:
        def sb(name, shape, dt=F32):
            return ctx.enter_context(nc.sbuf_tensor(name, list(shape), dt))

        def sig(name, per=1, credit=0):
            return Signal(ctx.enter_context(nc.semaphore(name)), per, credit)

        v = Buffers()
        bank = {n: ctx.enter_context(nc.psum_tensor(n, [P, 512], F32)) for n in ("pj0", "pj1", "pj2", "tr0", "tr1", "av")}
        v.sc = ctx.enter_context(nc.psum_tensor("sc", [P, 2, 512], F32))
        v.pj = [bank["pj0"], bank["pj1"], bank["pj2"]]
        v.tr = [bank["tr0"], bank["tr1"]]
        v.av = bank["av"]

        v.x = sb("x", [P, KC, B, ROW])
        v.mean_w = sb("mean_w", [P, P])
        v.ident = sb("ident", [P, P])
        v.ident16 = sb("ident16", [P, P], BF16)
        v.mask16 = sb("mask16", [P, 2, P], BF16)
        v.eps = sb("eps", [P, 1])
        v.gates = sb("gates", [P, 2])
        v.tanhs = sb("tanhs", [P, 2])
        v.wqkv = sb("wqkv", [P, CHUNKS, 2, KC, 512], F32R)
        v.ffw = sb("ffw", [P, KC * 2 * HID + PAIRS * D + HC * D])
        v.w1 = v.ffw[:, 0:KC * 2 * HID].rearrange("p (k n) -> p k n", k=KC)
        v.wo = v.ffw[:, KC * 2 * HID:KC * 2 * HID + PAIRS * D].rearrange("p (m n) -> p m n", m=PAIRS)
        v.w2 = v.ffw[:, KC * 2 * HID + PAIRS * D:].rearrange("p (c n) -> p c n", c=HC)
        v.small = sb("small", [P, 2 * HC + 3 * KC])
        v.b1c, v.b2c = v.small[:, 0:2 * HC], v.small[:, 2 * HC:2 * HC + KC]
        v.lng, v.lnb = v.small[:, 2 * HC + KC:2 * HC + 2 * KC], v.small[:, 2 * HC + 2 * KC:]
        v.qk_scale = sb("qk_scale", [P, 4 * DH])
        v.rotary = sb("rotary", [P, TILES, 4 * DH])
        v.table = sb("table", [P, TILES, 4 * DH])
        v.xs = sb("xs", [P, 2, 2, KC, P], F32R)
        v.sq = sb("sq", [P, 512])
        v.raw = sb("raw", [P, 2, 512])
        v.rot_b = sb("rot_b", [P, 2, 512])
        v.qk = sb("qk", [P, 4, 512])
        v.ss = sb("ss", [P, 32])
        v.nt = sb("nt", [P, 3, 32])
        v.rn = sb("rn", [P, 2, 32])
        v.qT = sb("qT", [P, PAIRS, P])
        v.kT = sb("kT", [P, 2, PAIRS, P])
        v.v_even = sb("v_even", [P, TILES, INNER])
        v.v_odd = sb("v_odd", [P, 2, INNER])
        v.mx = sb("mx", [P, 2, 4])
        v.nb = sb("nb", [P, 2, 4])
        v.probs = sb("probs", [P, 2, 512])
        v.psums = sb("psums", [P, 2, H])
        v.rs = sb("rs", [P, 2, 8])
        v.pT = sb("pT", [P, 2, 512])
        v.on = sb("on", [P, 2, 512])
        v.oT = sb("oT", [P, PAIRS, S])
        v.xc = sb("xc", [P, KC, S])
        v.gate = sb("gate", [P, 2, S])
        v.std = v.gate[:, 0, :]
        v.mask = v.gate[:, 1, 0:2 * P].rearrange("p (n j) -> p n j", n=2)
        v.hid = sb("hid", [P, HC, S])
        v.sqf = v.hid[:, 0:2, :]

        v.wx = v.ffw[:, 0:3968]
        v.whole = [v.ffw[:, 3968 + n * KC * 512:3968 + (n + 1) * KC * 512].rearrange("p (k n) -> p k n", k=KC) for n in range(2)]
        v.xw = [v.wx[:, n * KC * D:(n + 1) * KC * D].rearrange("p (k n) -> p k n", k=KC) for n in range(4)]
        v.ctxT = v.wx[:, 2048:2048 + KC * B * CTX].rearrange("p (k b c) -> p k b c", k=KC, b=B)
        v.ctx_b = v.wx[:, 2560:2560 + KC * 2 * CTX].rearrange("p (k e c) -> p k e c", k=KC, e=2)
        v.bv_row = v.wx[:, 2816:2816 + D]
        v.cols = v.wx[:, 3072:3072 + 3 * KC]
        v.bmask = v.wx[:, 3080:3088]
        v.mlp = v.wx[0:CTX, 3832:3832 + 133]
        v.w3_col, v.b3_col = v.wx[0:CTX, 3160:3161], v.wx[:, 3161:3162]
        v.w1s = v.wx[0:CTX, 3162:3165]
        v.w3w = v.wx[0:CTX, 3168:3168 + P]
        v.h1 = v.wx[0:CTX, 3300:3300 + XH]
        v.h2 = v.wx[0:CTX, 3320:3320 + XH]
        v.temp = v.wx[:, 3340:3340 + XH]
        v.feats = v.wx[:, 3360:3360 + TILES * 3 * XH].rearrange("p (t f h) -> p t f h", t=TILES, f=3)
        v.sums = v.wx[:, 3600:3600 + 4 * XH].rearrange("p (n h) -> p n h", n=4)
        v.xqT = v.qT[:, 0:8, :].rearrange("p a b -> p (a b)").rearrange("p (m s) -> p m s", m=KC)
        v.xkT = v.wx[:, 3700:3700 + KC * CTX].rearrange("p (m c) -> p m c", m=KC)
        v.kbd = v.kT[:, 0, :, :].rearrange("p a b -> p (a b)").rearrange("p (m h c) -> p m h c", m=KC, h=8)
        v.vbd = v.pT[:, :, :].rearrange("p a b -> p (a b)").rearrange("p (r n) -> p r n", r=8)
        v.dm = v.oT[:, :, :].rearrange("p a b -> p (a b)").rearrange("p (t h c) -> p t h c", t=TILES, h=XH)
        v.ex = v.probs[:, :, :].rearrange("p a b -> p (a b)").rearrange("p (h c) -> p h c", h=XH)
        v.ey = v.qk[:, 0:2, :].rearrange("p a b -> p (a b)").rearrange("p (h c) -> p h c", h=XH)
        v.ds_ = v.qk[:, 2:4, :].rearrange("p a b -> p (a b)").rearrange("p (h c) -> p h c", h=XH)
        v.at = v.on[:, :, :].rearrange("p a b -> p (a b)").rearrange("p (h c) -> p h c", h=XH)
        v.atT = v.v_even[:, :, :].rearrange("p a b -> p (a b)").rearrange("p (r s) -> p r s", r=8)
        v.xoT = v.hid[:, 2:4, :]
        v.ytmp = v.hid[:, 4:6, :]

        cross_attention(nc, a, sig, v)
        norm_between(nc, a, sig, v)
        stack(nc, a, sig, v)
        final(nc, a, sig, v)




def cross_attention(nc, a, sig, v):
    x, pj, tr, av, sc = v.x, v.pj, v.tr, v.av, v.sc
    LOADS = 0
    loaded = sig("a_loaded")
    setup = sig("a_setup")
    mean_ready, xc_ready, sq_ready, var_ready = sig("a_mean"), sig("a_xc", 2), sig("a_sq"), sig("a_var")
    std_ready, rstd_ready, xn_ready = sig("a_std"), sig("a_rstd"), sig("a_xn")
    ctx_ready, k_full, k_ready, kbd_ready = sig("a_ctx"), sig("a_kfull"), sig("a_k", 2), sig("a_kbd", 2)
    v_full, vbd_ready = sig("a_vfull"), sig("a_vbd", 4)
    q_full, q_ready = sig("a_qfull", 2), sig("a_q", 2)
    s_full, max_ready, dm_ready = sig("a_sfull", TILES), sig("a_max", TILES), sig("a_dm", TILES)
    e_ready, esum_ready, em_ready, e2_ready = sig("a_e", TILES), sig("a_esum", 2 * TILES), sig("a_em", TILES), sig("a_e2", TILES)
    f_step, f_ready, f_full = sig("a_fstep", 3 * TILES), sig("a_f", TILES), sig("a_ffull")
    h_step, h1_in, h1_ready, h2_full, h2_ready = sig("a_hstep", 2), sig("a_h1in"), sig("a_h1"), sig("a_h2full"), sig("a_h2")
    t_full, t_step, t_in, t_ready, t_half = sig("a_tfull"), sig("a_tstep"), sig("a_tin"), sig("a_t"), sig("a_thalf")
    ds_ready, p_ready, r_step, at_ready = sig("a_ds", TILES), sig("a_p", TILES), sig("a_rstep", 3 * TILES), sig("a_at", TILES)
    at_full, atT_ready = sig("a_atfull", TILES), sig("a_atT", 2 * TILES)
    o_full, o_ready, y_full, y_step, x_ready = sig("a_ofull", 2), sig("a_o", 2), sig("a_yfull", 2), sig("a_ystep", 2), sig("a_x", 2)
    whole_in = [sig("a_whole%d" % n, CHUNKS // 2 * 16) for n in range(2)]
    part_step, parts_ready = sig("a_partstep", 2 * CHUNKS), sig("a_parts", CHUNKS)
    parts_out = [sig("a_partsout%d" % c, 16) for c in range(CHUNKS)]
    loads = [
        (x[:, :, :, 1:ROW], a["xT"]), (v.mean_w[:], a["mean_w"]), (v.ident[:], a["ident"]), (v.mask, a["mask"]),
        (v.ctxT, a["ctxT"]), (v.bmask, a["bmask"]), (v.cols, a["cols"]), (v.mlp, a["mlp"]),
        (v.w3_col, a["w3"]), (v.rotary[:], a["rotary"]),
        (v.xw[0], a["Wq"]), (v.xw[1], a["Wk"]), (v.xw[2], a["Wv"]), (v.xw[3], a["Wo_x"]),
        (v.gates[:, 0:1], a["g_xattn"].partition_broadcast(P)), (v.gates[:, 1:2], a["g_ffn"].partition_broadcast(P)),
        (v.bv_row, a["bv"].partition_broadcast(P)), (v.b3_col, a["b3"].partition_broadcast(P)),
        (v.qk_scale[:], a["qk_scale"][0:1, :].rearrange("l n -> (l n)").partition_broadcast(P)),
    ]

    def all_loaded(eng):
        eng.wait_ge(loaded.sem, 16 * (len(loads) + 1))

    with nc.Block() as block:
        @block.sync
        def _(sp):
            for k in range(KC):
                sp.dma_start(x[:, k, :, 1:ROW], a["xT"][:, k, :, :]).then_inc(loaded.sem, 16)
            for dst, src in loads[1:]:
                sp.dma_start(dst, src).then_inc(loaded.sem, 16)
            all_loaded(sp)

            def load_whole(layer, c):
                sp.dma_start(v.whole[c % 2], a["Wqkv"][bass.ds(layer, 1), :, COLUMN[c]:COLUMN[c] + 512]
                             .rearrange("l (k p) n -> p (l k) n", p=P)).then_inc(whole_in[c % 2].sem, 16)
            def parts_to_dram(n, c):
                sp.wait_ge(parts_ready.sem, parts_ready.at(n - 1, c + 1))
                sp.dma_start(a["parts"][bass.ds(n, 1), c].rearrange("l p n -> p (l n)"),
                             v.wqkv[:, c].rearrange("p a k n -> p (a k n)").bitcast(F32)).then_inc(parts_out[c].sem, 16)
            load_whole(1, 0)
            load_whole(1, 1)
            with sp.Fori(1, DEPTH - 1) as n:
                for c in range(CHUNKS):
                    parts_to_dram(n, c)
                    load_whole(n + (c + 2) // CHUNKS, (c + 2) % CHUNKS)
            for c in range(CHUNKS):
                parts_to_dram(DEPTH - 1, c)
                load_whole(0 if c + 2 >= CHUNKS else DEPTH - 1, (c + 2) % CHUNKS)
            for c in range(CHUNKS - 2):
                sp.wait_ge(parts_ready.sem, parts_ready.at(DEPTH - 1, c + 1))
                load_whole(0, c + 2)
            for c in range(CHUNKS):
                sp.wait_ge(parts_out[c].sem, parts_out[c].at(DEPTH - 1, 0))

        @block.gpsimd
        def _(pool):
            pool.memset(x[:, :, :, 0:1], 0.0)
            pool.memset(v.eps[:], 1e-5)
            pool.memset(v.vbd, 0.0)
            pool.memset(v.v_even[:, 0, 0:1], 0.0)
            pool.drain().then_inc(setup.sem, 1)

            def split(n, c, first):
                pool.wait_ge(whole_in[c % 2].sem, whole_in[c % 2].at(n, 16 * (c // 2 + 1)))
                if not first:
                    pool.wait_ge(parts_out[c].sem, parts_out[c].at(n, 0))
                high, low = v.wqkv[:, c, 0], v.wqkv[:, c, 1]
                pool.nop().then_inc(part_step.sem, 1)
                pool.tensor_copy(high, v.whole[c % 2]).then_inc(part_step.sem, 1)
                pool.wait_ge(part_step.sem, part_step.at(n, 2 * c + 2))
                pool.tensor_tensor(low, v.whole[c % 2], high, ALU.subtract).then_inc(parts_ready.sem, 1)
            for c in range(CHUNKS):
                split(0, c, True)
            with pool.Fori(1, DEPTH) as n:
                for c in range(CHUNKS):
                    split(n, c, False)

        @block.tensor
        def _(pe):
            all_loaded(pe)
            pe.wait_ge(setup.sem, setup.at(0, 1))
            with pe.Fori(0, B) as b:
                def xrow(k):
                    return x[:, k, bass.ds(b, 1), 1:ROW].rearrange("p b s -> p (b s)")
                for k in range(KC):
                    mm = pe.matmul(pj[0][:], v.mean_w[:], xrow(k), start=(k == 0), stop=(k == KC - 1))
                mm.then_inc(mean_ready.sem, 1)
                for m in range(KC):
                    for k in range(KC):
                        mm = pe.matmul(pj[2][:, m * CTX:(m + 1) * CTX], v.xw[1][:, k, m * P:(m + 1) * P],
                                       v.ctxT[:, k, bass.ds(b, 1), :].rearrange("p b c -> p (b c)"),
                                       start=(k == 0), stop=(k == KC - 1))
                mm.then_inc(k_full.sem, 1)
                pe.wait_ge(ctx_ready.sem, ctx_ready.at(b, 1))
                for k in range(KC):
                    mm = pe.matmul(tr[0][:, 0:D], v.ctx_b[:, k, :, :].rearrange("p e c -> p (e c)"), v.xw[2][:, k, :],
                                   start=(k == 0), stop=(k == KC - 1))
                mm.then_inc(v_full.sem, 1)
                pe.wait_ge(sq_ready.sem, sq_ready.at(b, 1))
                for k in range(KC):
                    mm = pe.matmul(pj[1][:], v.mean_w[:], v.sqf[:, k, :], start=(k == 0), stop=(k == KC - 1))
                mm.then_inc(var_ready.sem, 1)
                pe.wait_ge(xn_ready.sem, xn_ready.at(b, 1))
                for m in range(KC):
                    for k in range(KC):
                        mm = pe.matmul(pj[m][:], v.xw[0][:, k, m * P:(m + 1) * P], v.xc[:, k, :],
                                       start=(k == 0), stop=(k == KC - 1))
                    mm.then_inc(q_full.sem, 1)
                pe.wait_ge(q_ready.sem, q_ready.at(b, 2))
                pe.wait_ge(kbd_ready.sem, kbd_ready.at(b, 2))
                for t in range(TILES):
                    if t > 0:
                        pe.wait_ge(dm_ready.sem, dm_ready.at(b, t))
                    for m in range(KC):
                        mm = pe.matmul(sc[:, m, :], v.xqT[:, m, t * P:(t + 1) * P],
                                       v.kbd[:, m, :, :].rearrange("p h c -> p (h c)"), start=True, stop=True)
                    mm.then_inc(s_full.sem, 1)
                    pe.wait_ge(f_ready.sem, f_ready.at(b, t + 1))
                    mm = pe.matmul(tr[1][:, 0:3 * XH], v.mean_w[:], v.feats[:, t, :, :].rearrange("p f h -> p (f h)"),
                                   start=(t == 0), stop=(t == TILES - 1))
                mm.then_inc(f_full.sem, 1)
                pe.wait_ge(h1_ready.sem, h1_ready.at(b, 1))
                pe.matmul(tr[1][:, 64:64 + XH], v.mlp[:, 4:4 + P], v.h1, start=True, stop=True).then_inc(h2_full.sem, 1)
                pe.wait_ge(h2_ready.sem, h2_ready.at(b, 1))
                pe.matmul(tr[1][:, 128:128 + XH], v.w3w, v.h2, start=True, stop=True).then_inc(t_full.sem, 1)
                for t in range(TILES):
                    pe.wait_ge(at_ready.sem, at_ready.at(b, t + 1))
                    if t > 0:
                        pe.wait_ge(atT_ready.sem, atT_ready.at(b, 2 * t))
                    for r in range(8):
                        mm = pe.transpose(tr[r // 4][:, (r % 4) * P:(r % 4 + 1) * P],
                                          v.at[:, 2 * r:2 * r + 2, :].rearrange("p h c -> p (h c)"), v.ident[:])
                    mm.then_inc(at_full.sem, 1)
                pe.wait_ge(atT_ready.sem, atT_ready.at(b, 2 * TILES))
                pe.wait_ge(vbd_ready.sem, vbd_ready.at(b, 4))
                for m in range(KC):
                    for r in range(4):
                        mm = pe.matmul(pj[m][:], v.vbd[:, 4 * m + r, :], v.atT[:, 4 * m + r, :], start=(r == 0), stop=(r == 3))
                    mm.then_inc(o_full.sem, 1)
                pe.wait_ge(o_ready.sem, o_ready.at(b, 2))
                for m in range(KC):
                    for k in range(KC):
                        mm = pe.matmul(sc[:, m, :], v.xw[3][:, k, m * P:(m + 1) * P], v.xoT[:, k, :],
                                       start=(k == 0), stop=(k == KC - 1))
                    mm.then_inc(y_full.sem, 1)

        @block.scalar
        def _(act):
            all_loaded(act)
            act.wait_ge(setup.sem, setup.at(0, 1))
            act.activation(v.tanhs[:], v.gates[:], ACT.Tanh).then_inc(setup.sem, 1)
            with act.Fori(0, B) as b:
                act.wait_ge(k_full.sem, k_full.at(b, 1))
                for m in range(KC):
                    act.activation(v.xkT[:, m, :], pj[2][:, m * CTX:(m + 1) * CTX], ACT.Identity,
                                   bias=v.cols[:, KC + m:KC + m + 1]).then_inc(k_ready.sem, 1)
                act.wait_ge(xc_ready.sem, xc_ready.at(b, 2))
                act.activation(v.sqf, v.xc[:], ACT.Square).then_inc(sq_ready.sem, 1)
                act.wait_ge(var_ready.sem, var_ready.at(b, 1))
                act.activation(v.std, pj[1][:], ACT.Sqrt, bias=v.eps[:]).then_inc(std_ready.sem, 1)
                for m in range(KC):
                    act.wait_ge(q_full.sem, q_full.at(b, m + 1))
                    act.activation(v.xqT[:, m, :], pj[m][:], ACT.Identity, bias=v.cols[:, m:m + 1]).then_inc(q_ready.sem, 1)
                for t in range(TILES):
                    act.wait_ge(dm_ready.sem, dm_ready.at(b, t + 1))
                    act.activation(v.ex, v.dm[:, t, :, :], ACT.Exp, scale=XD ** -0.5).then_inc(e_ready.sem, 1)
                    act.wait_ge(em_ready.sem, em_ready.at(b, t + 1))
                    act.activation(v.ey, v.ex, ACT.Square).then_inc(e2_ready.sem, 1)
                act.wait_ge(h1_in.sem, h1_in.at(b, 1))
                act.activation(v.h1, v.h1, ACT.Gelu, bias=v.mlp[:, 3:4]).then_inc(h1_ready.sem, 1)
                act.wait_ge(h2_full.sem, h2_full.at(b, 1))
                act.activation(v.h2, tr[1][0:CTX, 64:64 + XH], ACT.Gelu, bias=v.mlp[:, 132:133]).then_inc(h2_ready.sem, 1)
                act.wait_ge(t_in.sem, t_in.at(b, 1))
                act.activation(v.temp, v.temp, ACT.Exp, scale=-1.0).then_inc(t_ready.sem, 1)
                for t in range(TILES):
                    act.wait_ge(ds_ready.sem, ds_ready.at(b, t + 1))
                    act.activation(v.ex, v.ds_, ACT.Exp).then_inc(p_ready.sem, 1)
                    act.wait_ge(at_full.sem, at_full.at(b, t + 1))
                    for n in range(2):
                        act.activation(v.atT[:, 4 * n:4 * n + 4, t * P:(t + 1) * P],
                                       tr[n][:].rearrange("p (r q) -> p r q", r=4), ACT.Copy).then_inc(atT_ready.sem, 1)
                for m in range(KC):
                    act.wait_ge(o_full.sem, o_full.at(b, m + 1))
                    act.activation(v.xoT[:, m, :], pj[m][:], ACT.Copy).then_inc(o_ready.sem, 1)

        @block.vector
        def _(dve):
            all_loaded(dve)
            dve.wait_ge(setup.sem, setup.at(0, 2))
            for f, factor in enumerate((D * XD ** -0.5 / (S * CTX), D * XD ** -0.5 / S, D / (S * (CTX - 1.0)))):
                dve.tensor_scalar(v.w1s[:, f:f + 1], v.mlp[:, f:f + 1], factor, None, ALU.mult)
            dve.tensor_copy(v.w3w, bcast(v.w3_col, (CTX, P)))
            dve.tensor_copy(v.ident16[:], v.ident[:])
            dve.tensor_copy(v.mask16[:], v.mask).then_inc(setup.sem, 1)
            dve.wait_ge(setup.sem, setup.at(0, 3))
            with dve.Fori(0, B) as b:
                def xrow(k):
                    return x[:, k, bass.ds(b, 1), 1:ROW].rearrange("p b s -> p (b s)")
                dve.tensor_copy(v.ctx_b, bcast(v.ctxT[:, :, bass.ds(b, 1), :], (P, KC, 2, CTX))).then_inc(ctx_ready.sem, 1)
                dve.wait_ge(mean_ready.sem, mean_ready.at(b, 1))
                for k in range(KC):
                    dve.tensor_tensor(v.xc[:, k, :], xrow(k), pj[0][:], ALU.subtract).then_inc(xc_ready.sem, 1)
                dve.wait_ge(k_ready.sem, k_ready.at(b, 2))
                for m in range(KC):
                    dve.tensor_tensor(v.kbd[:, m, :, :], bcast(v.xkT[:, m:m + 1, :], (P, 8, CTX)),
                                      bcast(v.bmask.unsqueeze(2), (P, 8, CTX)), ALU.mult).then_inc(kbd_ready.sem, 1)
                dve.wait_ge(v_full.sem, v_full.at(b, 1))
                for m in range(KC):
                    for e in range(2):
                        rows = slice(e * CTX, (e + 1) * CTX)
                        src = tr[0][rows, m * P:(m + 1) * P].rearrange("p (r n) -> p r n", r=4)[:, :, e * XD:(e + 1) * XD]
                        row = v.bv_row[rows, m * P:(m + 1) * P].rearrange("p (r n) -> p r n", r=4)[:, :, e * XD:(e + 1) * XD]
                        dst = v.vbd[rows, 4 * m, e * XD:(e + 1) * XD]
                        dst = bass.AP(dst.tensor, dst.offset, [list(dst.ap[0]), [P + 2 * XD, 4], [1, XD]])
                        dve.tensor_tensor(dst, src, row, ALU.add).then_inc(vbd_ready.sem, 1)
                dve.wait_ge(std_ready.sem, std_ready.at(b, 1))
                dve.reciprocal(v.std, v.std).then_inc(rstd_ready.sem, 1)
                dve.wait_ge(rstd_ready.sem, rstd_ready.at(b, 1))
                dve.tensor_tensor(v.xc[:], v.xc[:], bcast(v.std.unsqueeze(1), (P, KC, S)), ALU.mult).then_inc(xn_ready.sem, 1)
                for t in range(TILES):
                    dve.wait_ge(s_full.sem, s_full.at(b, t + 1))
                    s4 = sc[:, :, :].rearrange("p m (h c) -> p (m h) c", c=CTX)
                    dve.tensor_reduce(v.feats[:, t, 0, :], s4, AX.X, ALU.add)
                    dve.tensor_reduce(v.feats[:, t, 1, :], s4, AX.X, ALU.max).then_inc(max_ready.sem, 1)
                    dve.wait_ge(max_ready.sem, max_ready.at(b, t + 1))
                    dve.tensor_tensor(v.dm[:, t, :, :], s4, bcast(v.feats[:, t, 1, :].unsqueeze(2), (P, XH, CTX)),
                                      ALU.subtract).then_inc(dm_ready.sem, 1)
                    dve.wait_ge(e_ready.sem, e_ready.at(b, t + 1))
                    dve.tensor_reduce(v.sums[:, 0, :], v.ex, AX.X, ALU.add).then_inc(esum_ready.sem, 1)
                    dve.wait_ge(esum_ready.sem, esum_ready.at(b, 2 * t + 1))
                    dve.tensor_scalar(v.sums[:, 1, :], v.sums[:, 0, :], 1.0 / CTX, None, ALU.mult)
                    dve.reciprocal(v.sums[:, 2, :], v.sums[:, 0, :]).then_inc(esum_ready.sem, 1)
                    dve.wait_ge(esum_ready.sem, esum_ready.at(b, 2 * t + 2))
                    dve.tensor_tensor(v.ex, v.ex, bcast(v.sums[:, 1, :].unsqueeze(2), (P, XH, CTX)),
                                      ALU.subtract).then_inc(em_ready.sem, 1)
                    dve.wait_ge(e2_ready.sem, e2_ready.at(b, t + 1))
                    dve.tensor_reduce(v.sums[:, 3, :], v.ey, AX.X, ALU.add).then_inc(f_step.sem, 1)
                    dve.wait_ge(f_step.sem, f_step.at(b, 3 * t + 1))
                    dve.tensor_tensor(v.sums[:, 3, :], v.sums[:, 3, :], v.sums[:, 2, :], ALU.mult).then_inc(f_step.sem, 1)
                    dve.wait_ge(f_step.sem, f_step.at(b, 3 * t + 2))
                    dve.tensor_tensor(v.feats[:, t, 2, :], v.sums[:, 3, :], v.sums[:, 2, :], ALU.mult).then_inc(f_step.sem, 1)
                    dve.wait_ge(f_step.sem, f_step.at(b, 3 * t + 3))
                    dve.nop().then_inc(f_ready.sem, 1)
                dve.wait_ge(f_full.sem, f_full.at(b, 1))
                dve.tensor_scalar(v.h1, tr[1][0:CTX, 0:XH], v.w1s[:, 0:1], None, ALU.mult).then_inc(h_step.sem, 1)
                dve.wait_ge(h_step.sem, h_step.at(b, 1))
                dve.scalar_tensor_tensor(v.h1, tr[1][0:CTX, XH:2 * XH], v.w1s[:, 1:2], v.h1, ALU.mult, ALU.add).then_inc(h_step.sem, 1)
                dve.wait_ge(h_step.sem, h_step.at(b, 2))
                dve.scalar_tensor_tensor(v.h1, tr[1][0:CTX, 2 * XH:3 * XH], v.w1s[:, 2:3], v.h1, ALU.mult, ALU.add).then_inc(h1_in.sem, 1)
                dve.wait_ge(t_full.sem, t_full.at(b, 1))
                dve.tensor_scalar(v.temp, tr[1][:, 128:128 + XH], v.b3_col, float(np.float32(np.log(0.1))), ALU.add, ALU.max).then_inc(t_step.sem, 1)
                dve.wait_ge(t_step.sem, t_step.at(b, 1))
                dve.tensor_scalar(v.temp, v.temp, float(np.float32(np.log(10.0))), None, ALU.min).then_inc(t_in.sem, 1)
                dve.wait_ge(t_ready.sem, t_ready.at(b, 1))
                dve.tensor_scalar(v.temp, v.temp, 0.5, None, ALU.mult).then_inc(t_half.sem, 1)
                dve.wait_ge(t_half.sem, t_half.at(b, 1))
                for t in range(TILES):
                    dve.tensor_tensor(v.ds_, v.dm[:, t, :, :], bcast(v.temp.unsqueeze(2), (P, XH, CTX)), ALU.mult).then_inc(ds_ready.sem, 1)
                    dve.wait_ge(p_ready.sem, p_ready.at(b, t + 1))
                    dve.tensor_reduce(v.sums[:, 0, :], v.ex, AX.X, ALU.add).then_inc(r_step.sem, 1)
                    dve.wait_ge(r_step.sem, r_step.at(b, 3 * t + 1))
                    dve.reciprocal(v.sums[:, 1, :], v.sums[:, 0, :]).then_inc(r_step.sem, 1)
                    dve.wait_ge(r_step.sem, r_step.at(b, 3 * t + 2))
                    dve.tensor_scalar(v.sums[:, 2, :], v.sums[:, 1, :], 0.0, None, ALU.max).then_inc(r_step.sem, 1)
                    dve.wait_ge(r_step.sem, r_step.at(b, 3 * t + 3))
                    if t > 0:
                        dve.wait_ge(at_full.sem, at_full.at(b, t))
                    dve.scalar_tensor_tensor(v.at, v.ex, 0.0, bcast(v.sums[:, 2, :].unsqueeze(2), (P, XH, CTX)),
                                             ALU.max, ALU.mult).then_inc(at_ready.sem, 1)
                for m in range(KC):
                    dve.wait_ge(y_full.sem, y_full.at(b, m + 1))
                    dve.tensor_scalar(v.ytmp[:, m, :], sc[:, m, :], v.cols[:, 2 * KC + m:2 * KC + m + 1], v.tanhs[:, 0:1],
                                      ALU.add, ALU.mult).then_inc(y_step.sem, 1)
                    dve.wait_ge(y_step.sem, y_step.at(b, m + 1))
                    dve.tensor_tensor(xrow(m), xrow(m), v.ytmp[:, m, :], ALU.add).then_inc(x_ready.sem, 1)


def norm_between(nc, a, sig, v):
    x, pj = v.x, v.pj
    kept, mean_ready, xc_ready, sq_ready, var_ready = sig("n_kept"), sig("n_mean"), sig("n_xc", 2), sig("n_sq"), sig("n_var")
    std_ready, rstd_ready, x_ready, zero = sig("n_std"), sig("n_rstd"), sig("n_x", 2), sig("n_zero")
    with nc.Block() as block:
        @block.sync
        def _(sp):
            for k in range(KC):
                sp.dma_start(a["kept"][:, k, :, :], x[:, k, :, 1:ROW]).then_inc(kept.sem, 16)
            sp.wait_ge(kept.sem, 16 * KC)

        @block.gpsimd
        def _(pool):
            pool.memset(v.v_even[:, 0, :], 0.0).then_inc(zero.sem, 1)

        @block.tensor
        def _(pe):
            with pe.Fori(0, B) as b:
                for k in range(KC):
                    mm = pe.matmul(pj[0][:], v.mean_w[:], x[:, k, bass.ds(b, 1), 1:ROW].rearrange("p b s -> p (b s)"),
                                   start=(k == 0), stop=(k == KC - 1))
                mm.then_inc(mean_ready.sem, 1)
                pe.wait_ge(sq_ready.sem, sq_ready.at(b, 1))
                for k in range(KC):
                    mm = pe.matmul(pj[1][:], v.mean_w[:], v.sqf[:, k, :], start=(k == 0), stop=(k == KC - 1))
                mm.then_inc(var_ready.sem, 1)

        @block.scalar
        def _(act):
            with act.Fori(0, B) as b:
                act.wait_ge(xc_ready.sem, xc_ready.at(b, 2))
                act.activation(v.sqf, v.xc[:], ACT.Square).then_inc(sq_ready.sem, 1)
                act.wait_ge(var_ready.sem, var_ready.at(b, 1))
                act.activation(v.std, pj[1][:], ACT.Sqrt, bias=v.eps[:]).then_inc(std_ready.sem, 1)

        @block.vector
        def _(dve):
            dve.wait_ge(kept.sem, 16 * KC)
            with dve.Fori(0, B) as b:
                def xrow(k):
                    return x[:, k, bass.ds(b, 1), 1:ROW].rearrange("p b s -> p (b s)")
                dve.wait_ge(mean_ready.sem, mean_ready.at(b, 1))
                for k in range(KC):
                    dve.tensor_tensor(v.xc[:, k, :], xrow(k), pj[0][:], ALU.subtract).then_inc(xc_ready.sem, 1)
                dve.wait_ge(std_ready.sem, std_ready.at(b, 1))
                dve.reciprocal(v.std, v.std).then_inc(rstd_ready.sem, 1)
                dve.wait_ge(rstd_ready.sem, rstd_ready.at(b, 1))
                for k in range(KC):
                    dve.tensor_tensor(xrow(k), v.xc[:, k, :], v.std, ALU.mult).then_inc(x_ready.sem, 1)
                dve.wait_ge(x_ready.sem, x_ready.at(b, 2))


def steps_of(first, ffn, following):
    out = []

    def tail(g, kinds="VA"):
        for kind, back in (("V", 1), ("A", 2)):
            t, c = divmod(g - back, 4)
            if kind not in kinds or (first and t < 0):
                continue
            out.append((kind, t, c))
            if kind == "A" and c % 2 == 1:
                out.append(("O", t, c // 2))
            if kind == "A" and c % 2 == 0 and not (first and g - back < 2):
                t, c = divmod(g - back - 1, 4)
                out.append(("X", t, c // 2))

    for t in range(TILES):
        proj = [("P", t + 1, c) for c in range(6)] if t + 1 < TILES or following else []
        turn = [("T", t + 1, g) for g in range(4)] if proj else []
        norm = [("N", t + 1, 0)] if proj else []
        extra = {}
        if ffn:
            extra = {(0, 3): [("W", 0, 0), ("W", 0, 1)], (1, 1): [("M", 0, 0)], (2, 1): [("Y", 0, 0)], (2, 3): [("Y", 0, 1)]}
        block = ffn and t == 1
        for k in range(4):
            out.append(("S", t, k))
            if k < 2:
                out += proj[2 * k:2 * k + 1]
                tail(4 * t + k)
                out += extra.get((t, k), []) + proj[2 * k + 1:2 * k + 2]
            elif k == 2:
                out += proj[4:5]
                tail(4 * t + k)
                out += norm
            elif block:
                tail(4 * t + k)
                out.append(("R", 0, 0))
                out += turn + proj[5:6]
                tail(4 * t + 4)
                for c in range(HC):
                    out.append(("G", 0, c))
                    if c == 1:
                        tail(4 * t + 5, "A")
                    out.append(("U", 0, c))
            else:
                out += extra.get((t, k), [])
                tail(4 * t + k)
                out += turn + proj[5:6]
    seen, once = set(), []
    for step in out:
        if step not in seen:
            once.append(step)
        seen.add(step)
    return once


def closing_steps():
    out = [("V", -1, 3), ("A", -1, 2), ("X", -1, 0), ("A", -1, 3), ("O", -1, 1), ("X", -1, 1)]
    return out + FFN_ORDER


FFN_ORDER = [("W", 0, 0), ("W", 0, 1), ("M", 0, 0), ("R", 0, 0)] + [(k, 0, c) for c in range(HC) for k in "GU"] + [("Y", 0, 0), ("Y", 0, 1)]
RINGS = {"P": "pj", "W": "pj", "M": "pj", "R": "pj", "G": "pj", "U": "pj", "Y": "pj", "T": "tr", "V": "tr", "X": "tr", "S": "sc"}
SIZE = {"pj": 3, "tr": 2, "sc": 2}
PRELUDE = [("P", 0, c) for c in range(6)] + [("N", 0, 0)] + [("T", 0, g) for g in range(4)]


def ring_plan(steps, before, shift, taken):
    plan = {}
    for ring, size in SIZE.items():
        uses = [(s, 0) for s in steps if RINGS.get(s[0]) == ring]
        past = [(s, -shift) for s in before if RINGS.get(s[0]) == ring][-size:]
        both = past + uses
        for n, (s, _) in enumerate(uses):
            old = n + len(past) - size
            plan[s] = ((n + taken[ring]) % size, both[old] if old >= 0 else None)
    return plan


def stack(nc, a, sig, v):
    x, pj, tr, av, sc = v.x, v.pj, v.tr, v.av, v.sc
    DONE = B * 2
    xs_ready, xs_high = sig("xs_ready", 4), sig("xs_high")
    pj_full = sig("pj_full", 6, credit=12)
    sq_ready = sig("sq_ready", 4)
    raw_ready = sig("raw_ready", 4)
    cos_ready = sig("cos_ready", 4, credit=2)
    rot_ready = sig("rot_ready", 4)
    ss_ready = sig("ss_ready", 4, credit=2)
    newton = sig("newton", 3 + 3 * NEWTON)
    rn_ready = sig("rn_ready", 2)
    sum_ready = sig("sum_ready", 4, credit=2)
    kn_ready = sig("kn_ready", 2)
    qk_full = sig("qk_full", 4, credit=4)
    qk_ready = sig("qk_ready", 4)
    v_ready = sig("v_ready", 2)
    s_full = sig("s_full", 4, credit=4)
    mx_ready = sig("mx_ready", 4)
    nb_ready = sig("nb_ready", 4)
    p_ready = sig("p_ready", 4, credit=8)
    pT_full = sig("pT_full", 4, credit=2)
    pT_ready = sig("pT_ready", 4)
    av_full = sig("av_full", 4, credit=8)
    rs_ready = sig("rs_ready", 2)
    on_ready = sig("on_ready", 2, credit=2)
    oT_full = sig("oT_full", 2, credit=2)
    oT_ready = sig("oT_ready", 2)
    table_ready = sig("table_ready", 1)
    f_full = sig("f_full", 6 + 2 * HC, credit=18)
    xa_ready = sig("xa_ready", 2)
    xc_ready = sig("xc_ready", 2)
    sqf_ready = sig("sqf_ready", 1)
    std_ready = sig("std_ready", 1)
    rstd_ready = sig("rstd_ready", 1)
    xm_ready = sig("xm_ready", 1)
    xn_ready = sig("xn_ready", 2)
    gate_ready = sig("gate_ready", HC)
    hid_ready = sig("hid_ready", HC, credit=2)
    x_ready = sig("x_ready", 2, credit=DONE)
    wqkv_loaded = [sig("wqkv_loaded%d" % c, 16, credit=16) for c in range(CHUNKS)]
    scale_loaded = sig("scale_loaded", 16, credit=16)
    ffn_loaded = sig("ffn_loaded", FFN_LOADS * 16)

    def f_count(step):
        return FFN_ORDER.index(step) + 1

    def freed(step):
        kind, t, c = step
        if kind == "P":
            return (raw_ready, c + 1) if c < 4 else (v_ready, c - 3)
        return {"T": (qk_ready, c + 1), "V": (pT_ready, c + 1), "X": (oT_ready, c + 1), "S": (p_ready, c + 1),
                "W": (xa_ready, c + 1), "M": (xc_ready, 2), "R": (std_ready, 1), "G": (gate_ready, c + 1),
                "U": (hid_ready, c + 1), "Y": (x_ready, c + 1)}[kind]

    def bank_free(i, past):
        old, back = past
        signal, n = freed(old)
        return signal.sem, signal.at(unit(i, old, back), n)

    def unit(i, step, back=0):
        if step[0] in "WMRGUY":
            return i - 1 + back
        return (i + back) * TILES + step[1]

    opening = steps_of(True, False, True)
    body = steps_of(False, True, True)
    last = steps_of(False, True, False)
    phases = []
    taken = dict.fromkeys(SIZE, 0)
    before = []
    for begin, count, steps, shift in ((0, 1, PRELUDE, 0), (0, 1, opening, 0), (1, 1, body, 1), (2, ITERS - 3, body, 1),
                                       (ITERS - 1, 1, last, 1), (ITERS, 1, closing_steps(), 1)):
        phases.append((begin, count, steps, ring_plan(steps, before, shift, taken)))
        for ring in SIZE:
            used = sum(RINGS.get(kind) == ring for kind, _, _ in steps)
            assert count == 1 or used % SIZE[ring] == 0
            taken[ring] += used * count
        before = steps

    def run(eng, engine, do):
        def emit(i, steps, plan):
            for step in steps:
                slot, past = plan.get(step, (None, None))
                do(i, step, slot, past)
        for first, count, steps, plan in phases:
            if count == 1:
                emit(first, steps, plan)
            else:
                with eng.Fori(first, first + count) as i:
                    emit(i, steps, plan)

    def head(c, n):
        return 8 * (c // 2) + 2 * n + c % 2

    def row(i, step):
        return (i + step[1] // TILES) % B if step[0] not in "WMRGUY" else (i - 1) % B

    def layer(i, step):
        return (i + step[1] // TILES) // B if step[0] not in "WMRGUY" else (i - 1) // B

    def xrow(k, b, lo=1):
        return x[:, k, bass.ds(b, 1), lo:lo + S].rearrange("p b s -> p (b s)")

    with nc.Block() as block:
        @block.sync
        def _(sp):
            def load_ffn(l):
                def src(name):
                    return a[name][bass.ds(l, 1)]
                sp.dma_start(v.wo[:], src("Wo").rearrange("l (c p) n -> p (l c) n", p=P)).then_inc(ffn_loaded.sem, 16)
                for k in range(KC):
                    sp.dma_start(v.w1[:, k, :], src("W1")[:, k * P:(k + 1) * P, :].rearrange("l p n -> p (l n)")).then_inc(ffn_loaded.sem, 16)
                sp.dma_start(v.w2[:, 0:HC - 1, :], src("W2")[:, 0:(HC - 1) * P, :].rearrange("l (c p) n -> p (l c) n", p=P)).then_inc(ffn_loaded.sem, 16)
                sp.dma_start(v.w2[0:LAST, HC - 1, :], src("W2")[:, (HC - 1) * P:HID, :].rearrange("l p n -> p (l n)")).then_inc(ffn_loaded.sem, 16)
                sp.dma_start(v.small[:], src("small").rearrange("l p n -> p (l n)")).then_inc(ffn_loaded.sem, 16)

            def load_chunk(l, c):
                sp.dma_start(v.wqkv[:, c].rearrange("p a k n -> p (a k n)").bitcast(F32),
                             a["parts"][bass.ds(l, 1), c].rearrange("l p n -> p (l n)")).then_inc(wqkv_loaded[c].sem, 16)

            def load_scale(l):
                sp.dma_start(v.qk_scale[:], a["qk_scale"][bass.ds(l, 1), :].rearrange("l n -> (l n)").partition_broadcast(P)).then_inc(scale_loaded.sem, 16)
            for c in range(CHUNKS):
                sp.drain().then_inc(wqkv_loaded[c].sem, wqkv_loaded[c].credit)
            sp.drain().then_inc(scale_loaded.sem, scale_loaded.credit)
            load_ffn(0)
            with sp.Fori(1, DEPTH) as l:
                sp.wait_ge(table_ready.sem, table_ready.at(l * B, 0))
                load_scale(l)
                for c in range(CHUNKS):
                    sp.wait_ge(pj_full.sem, pj_full.at(l * (B * TILES) - 1, c + 1))
                    load_chunk(l, c)
                sp.wait_ge(x_ready.sem, x_ready.at(l * B, 0))
                load_ffn(l)

        @block.gpsimd
        def _(pool):
            pool.drain().then_inc(sum_ready.sem, sum_ready.credit)
            pool.drain().then_inc(cos_ready.sem, cos_ready.credit)
            def do(i, step, slot, past):
                kind, t, c = step
                if kind == "P":
                    tau = unit(i, step)
                    if c == 0:
                        b = row(i, step)
                        pool.wait_ge(x_ready.sem, x_ready.at(i + t // TILES - B, 2))
                        pool.wait_ge(pj_full.sem, pj_full.at(tau - 2, 6))
                        def cols(k):
                            lo = 1 - k + (t % TILES) * P
                            return x[:, k, bass.ds(b, 1), lo:lo + P].rearrange("p b s -> p (b s)")
                        for k in range(KC):
                            pool.tensor_copy(v.xs[:, t % 2, 0, k, :], cols(k)).then_inc(xs_ready.sem, 1)
                        pool.wait_ge(xs_ready.sem, xs_ready.at(tau, KC))
                        pool.nop().then_inc(xs_high.sem, 1)
                        for k in range(KC):
                            pool.tensor_tensor(v.xs[:, t % 2, 1, k, :], cols(k), v.xs[:, t % 2, 0, k, :], ALU.subtract).then_inc(xs_ready.sem, 1)
                    if c < 4:
                        pool.wait_ge(raw_ready.sem, raw_ready.at(tau, c + 1))
                        pool.wait_ge(qk_full.sem, qk_full.at(tau - 1, c + 1))
                        base = 2 * DH * (c % 2)
                        cos = v.table[:, t % TILES:t % TILES + 1, base:base + DH]
                        q3 = v.qk[:, c, :].rearrange("p (h d) -> p h d", h=8)
                        if c == 0 and t % TILES == 0:
                            pool.wait_ge(table_ready.sem, table_ready.at(i + t // TILES, 1))
                        pool.tensor_tensor(q3, v.raw[:, c % 2, :].rearrange("p (h d) -> p h d", h=8), bcast(cos, (P, 8, DH)),
                                           ALU.mult).then_inc(cos_ready.sem, 1)
                        pool.wait_ge(cos_ready.sem, cos_ready.at(tau, c + 1))
                        pool.wait_ge(rot_ready.sem, rot_ready.at(tau, c + 1))
                        pool.tensor_tensor(v.qk[:, c, :], v.qk[:, c, :], v.rot_b[:, c % 2, :], ALU.add).then_inc(sum_ready.sem, 1)
                if kind == "N":
                    tau = unit(i, step)
                    pool.wait_ge(rn_ready.sem, rn_ready.at(tau, 1))
                    for g in range(2):
                        pool.wait_ge(sum_ready.sem, sum_ready.at(tau, 2 * g + 2))
                        k3 = v.qk[:, 2 * g + 1, :].rearrange("p (h d) -> p h d", h=8)
                        r3 = v.rn[:, t % 2, 16 * g + 8:16 * g + 16].unsqueeze(2)
                        pool.tensor_tensor(k3, k3, bcast(r3, (P, 8, DH)), ALU.mult).then_inc(kn_ready.sem, 1)
            run(pool, "pool", do)

        @block.tensor
        def _(pe):
            pe.drain().then_inc(pj_full.sem, pj_full.credit)
            pe.drain().then_inc(qk_full.sem, qk_full.credit)
            pe.drain().then_inc(av_full.sem, av_full.credit)
            pe.drain().then_inc(s_full.sem, s_full.credit)
            pe.drain().then_inc(pT_full.sem, pT_full.credit)
            pe.drain().then_inc(f_full.sem, f_full.credit)
            pe.drain().then_inc(oT_full.sem, oT_full.credit)
            def do(i, step, slot, past):
                kind, t, c = step
                u = unit(i, step)
                ts = t % TILES
                if kind == "P":
                    if c == 0:
                        pe.wait_ge(xs_ready.sem, xs_ready.at(u, 4))
                    if ts == 0:
                        pe.wait_ge(wqkv_loaded[c].sem, wqkv_loaded[c].at(layer(i, step), 0))
                    if past:
                        pe.wait_ge(*bank_free(i, past))
                    products = [(0, 0), (0, 1), (1, 0)]
                    for n, (xp, wp) in enumerate(products):
                        for k in range(KC):
                            mm = pe.matmul(pj[slot][:], v.xs[:, t % 2, xp, k, :], v.wqkv[:, c, wp, k, :],
                                           start=(n == 0 and k == 0), stop=(n == 2 and k == KC - 1))
                    mm.then_inc(pj_full.sem, 1)
                if kind == "T":
                    if c % 2 == 0:
                        pe.wait_ge(sum_ready.sem, sum_ready.at(u, c + 1))
                    else:
                        pe.wait_ge(kn_ready.sem, kn_ready.at(u, c // 2 + 1))
                    if past:
                        pe.wait_ge(*bank_free(i, past))
                    for n in range(4):
                        mm = pe.transpose(tr[slot][:, n * P:(n + 1) * P], v.qk[:, c, n * P:(n + 1) * P], v.ident[:])
                    mm.then_inc(qk_full.sem, 1)
                if kind == "S":
                    pe.wait_ge(qk_ready.sem, qk_ready.at(u, 2 * (c // 2) + 2))
                    if past:
                        pe.wait_ge(*bank_free(i, past))
                    out = sc[:, slot, :]
                    first = ts == 0
                    pe.matmul(out, v.ident16[:], bcast(v.mask16[:, 0:1, :] if first else v.mask16[:, 1:2, :], (P, 4, P)),
                              start=True, stop=False, skip_group_check=True)
                    for n in range(4):
                        h = head(c, n)
                        r = slice(DH * (h % 2), DH * (h % 2) + DH)
                        q, kc, kp = v.qT[r, h // 2, :], v.kT[r, t % 2, h // 2, :], v.kT[r, 1 - t % 2, h // 2, :]
                        o = n * P
                        if not first:
                            pe.matmul(sc[0:W, slot, o + W:o + P], q[:, 0:W], kp[:, W:P], start=False, stop=False, skip_group_check=True)
                        pe.matmul(sc[0:W, slot, o:o + W], q[:, 0:W], kc[:, 0:W], start=False, stop=False, skip_group_check=True)
                        mm = pe.matmul(sc[W:P, slot, o:o + P], q[:, W:P], kc, start=False, stop=(n == 3), skip_group_check=True)
                    mm.then_inc(s_full.sem, 1)
                if kind == "V":
                    pe.wait_ge(p_ready.sem, p_ready.at(u, c + 1))
                    if past:
                        pe.wait_ge(*bank_free(i, past))
                    for n in range(4):
                        mm = pe.transpose(tr[slot][:, n * P:(n + 1) * P], v.probs[:, c % 2, n * P:(n + 1) * P], v.ident[:])
                    mm.then_inc(pT_full.sem, 1)
                if kind == "A":
                    pe.wait_ge(pT_ready.sem, pT_ready.at(u, c + 1))
                    pe.wait_ge(v_ready.sem, v_ready.at(u, c // 2 + 1))
                    if c % 2 == 0:
                        pe.wait_ge(on_ready.sem, on_ready.at(u, c // 2))
                    for n in range(4):
                        h = head(c, n)
                        o = (h % 8) * DH
                        pe.matmul(av[0:W, o:o + DH], v.pT[:, c % 2, n * P:n * P + W], v.v_even[:, ts, h * DH:(h + 1) * DH], start=True, stop=True)
                        mm = pe.matmul(av[W:P, o:o + DH], v.pT[:, c % 2, n * P + W:(n + 1) * P], v.v_odd[:, t % 2, h * DH:(h + 1) * DH], start=True, stop=True)
                    mm.then_inc(av_full.sem, 1)
                if kind == "X":
                    pe.wait_ge(on_ready.sem, on_ready.at(u, c + 1))
                    if past:
                        pe.wait_ge(*bank_free(i, past))
                    for n in range(4):
                        mm = pe.transpose(tr[slot][:, n * P:(n + 1) * P], v.on[:, c, n * P:(n + 1) * P], v.ident[:])
                    mm.then_inc(oT_full.sem, 1)
                if kind == "W":
                    if c == 0:
                        pe.wait_ge(oT_ready.sem, oT_ready.at((u + 1) * TILES, 0))
                        pe.wait_ge(ffn_loaded.sem, ffn_loaded.at(layer(i, step), FFN_LOADS * 16))
                    if past:
                        pe.wait_ge(*bank_free(i, past))
                    for n in range(PAIRS):
                        mm = pe.matmul(pj[slot][:], v.wo[:, n, c * P:(c + 1) * P], v.oT[:, n, :], start=(n == 0), stop=(n == PAIRS - 1))
                if kind == "M":
                    pe.wait_ge(xa_ready.sem, xa_ready.at(u, 2))
                    if past:
                        pe.wait_ge(*bank_free(i, past))
                    for k in range(KC):
                        mm = pe.matmul(pj[slot][:], v.mean_w[:], xrow(k, row(i, step), 1 - k), start=(k == 0), stop=(k == KC - 1))
                if kind == "R":
                    pe.wait_ge(sqf_ready.sem, sqf_ready.at(u, 1))
                    if past:
                        pe.wait_ge(*bank_free(i, past))
                    for k in range(KC):
                        mm = pe.matmul(pj[slot][:], v.mean_w[:], v.sqf[:, k, :], start=(k == 0), stop=(k == KC - 1))
                if kind in "GU":
                    n = P if c < HC - 1 else LAST
                    col = c * P + (HID if kind == "G" else 0)
                    if kind == "G" and c == 0:
                        pe.wait_ge(xn_ready.sem, xn_ready.at(u, 2))
                    if past:
                        pe.wait_ge(*bank_free(i, past))
                    for k in range(KC):
                        mm = pe.matmul(pj[slot][0:n, :], v.w1[:, k, col:col + n], v.xc[:, k, :], start=(k == 0), stop=(k == KC - 1))
                if kind == "Y":
                    pe.wait_ge(hid_ready.sem, hid_ready.at(u, HC))
                    if past:
                        pe.wait_ge(*bank_free(i, past))
                    for n in range(HC):
                        r = P if n < HC - 1 else LAST
                        mm = pe.matmul(pj[slot][:], v.w2[0:r, n, c * P:(c + 1) * P], v.hid[0:r, n, :], start=(n == 0), stop=(n == HC - 1))
                if kind in "WMRGUY":
                    mm.then_inc(f_full.sem, 1)
            run(pe, "pe", do)

        @block.scalar
        def _(act):
            act.drain().then_inc(p_ready.sem, p_ready.credit)
            def do(i, step, slot, past):
                kind, t, c = step
                u = unit(i, step)
                ts = t % TILES
                if kind == "P":
                    act.wait_ge(pj_full.sem, pj_full.at(u, c + 1))
                if kind == "P" and c < 4:
                    act.wait_ge(ss_ready.sem, ss_ready.at(u, c - 1))
                    act.wait_ge(cos_ready.sem, cos_ready.at(u, c - 1))
                    act.activation(v.raw[:, c % 2, :], pj[slot][:], ACT.Copy).then_inc(raw_ready.sem, 1)
                    act.wait_ge(raw_ready.sem, raw_ready.at(u, c + 1))
                    act.wait_ge(ss_ready.sem, ss_ready.at(u, c))
                    act.activation(v.sq[:], v.raw[:, c % 2, :], ACT.Square).then_inc(sq_ready.sem, 1)
                if kind == "P" and c >= 4:
                    cs = slice((c - 4) * 512, (c - 3) * 512)
                    act.wait_ge(av_full.sem, av_full.at(u - 2, 4))
                    act.activation(v.v_odd[:, t % 2, cs], pj[slot][:], ACT.Copy)
                    if ts < TILES - 1:
                        act.activation(v.v_even[W:P, ts + 1, cs], pj[slot][W:P, :], ACT.Copy)
                    act.activation(v.v_even[0:W, ts, cs], pj[slot][0:W, :], ACT.Copy).then_inc(v_ready.sem, 1)
                if kind == "T":
                    act.wait_ge(qk_full.sem, qk_full.at(u, c + 1))
                    act.wait_ge(s_full.sem, s_full.at(u - 1, 4))
                    hp = slice(4 * (c // 2), 4 * (c // 2) + 4)
                    dst = v.qT[:, hp, :] if c % 2 == 0 else v.kT[:, t % 2, hp, :]
                    act.activation(dst, tr[slot][:].rearrange("p (n q) -> p n q", n=4), ACT.Copy).then_inc(qk_ready.sem, 1)
                if kind == "S":
                    act.wait_ge(nb_ready.sem, nb_ready.at(u, c + 1))
                    act.wait_ge(pT_full.sem, pT_full.at(u, c - 1))
                    for n in range(4):
                        h = head(c, n)
                        col = 16 * (h // 8) + h % 8
                        e = act.activation(v.probs[:, c % 2, n * P:(n + 1) * P], sc[:, slot, n * P:(n + 1) * P], ACT.Exp,
                                           bias=v.nb[:, c % 2, n:n + 1], scale=v.rn[:, t % 2, col:col + 1],
                                           accum_out=v.psums[:, t % 2, h:h + 1])
                    e.then_inc(p_ready.sem, 1)
                if kind == "X":
                    act.wait_ge(oT_full.sem, oT_full.at(u, c + 1))
                    if ts == 0 and c == 0:
                        act.wait_ge(f_full.sem, f_full.at(i - 1, 2))
                    act.activation(v.oT[:, 4 * c:4 * c + 4, ts * P:(ts + 1) * P], tr[slot][:].rearrange("p (n q) -> p n q", n=4),
                                   ACT.Copy).then_inc(oT_ready.sem, 1)
                if kind == "R":
                    act.wait_ge(f_full.sem, f_full.at(u, f_count(step)))
                    act.activation(v.std, pj[slot][:], ACT.Sqrt, bias=v.eps[:]).then_inc(std_ready.sem, 1)
                if kind == "M":
                    act.wait_ge(xc_ready.sem, xc_ready.at(u, 2))
                    act.activation(v.sqf, v.xc[:], ACT.Square).then_inc(sqf_ready.sem, 1)
                if kind == "G":
                    n = P if c < HC - 1 else LAST
                    act.wait_ge(f_full.sem, f_full.at(u, f_count(step)))
                    act.wait_ge(hid_ready.sem, hid_ready.at(u, c - 1))
                    act.activation(v.gate[0:n, c % 2, :], pj[slot][0:n, :], ACT.Gelu, bias=v.b1c[0:n, HC + c:HC + c + 1]).then_inc(gate_ready.sem, 1)
            run(act, "act", do)

        @block.vector
        def _(dve):
            dve.drain().then_inc(x_ready.sem, x_ready.credit)
            dve.drain().then_inc(hid_ready.sem, hid_ready.credit)
            dve.drain().then_inc(ss_ready.sem, ss_ready.credit)
            dve.drain().then_inc(on_ready.sem, on_ready.credit)

            def do(i, step, slot, past):
                kind, t, c = step
                u = unit(i, step)
                ts = t % TILES
                if kind == "P" and c == 0 and ts == 0:
                    pair = i + t // TILES
                    dve.wait_ge(scale_loaded.sem, scale_loaded.at(layer(i, step), 0))
                    dve.tensor_tensor(v.table[:], v.rotary[:], bcast(v.qk_scale[:].unsqueeze(1), (P, TILES, 4 * DH)), ALU.mult).then_inc(table_ready.sem, 1)
                    dve.wait_ge(table_ready.sem, table_ready.at(pair, 1))
                if kind == "P" and c < 4:
                    dve.wait_ge(raw_ready.sem, raw_ready.at(u, c + 1))
                    dve.wait_ge(sum_ready.sem, sum_ready.at(u, c - 1))
                    src = v.raw[:, c % 2, :].rearrange("p (h d) -> p h d", h=8)
                    base = 2 * DH * (c % 2)
                    sin = v.table[:, ts:ts + 1, base + DH:base + 2 * DH]
                    dst_b = v.rot_b[:, c % 2, :].rearrange("p (h d) -> p h d", h=8)
                    hf = DH // 2
                    dve.tensor_tensor(dst_b[:, :, 0:hf], src[:, :, hf:DH], bcast(sin[:, :, 0:hf], (P, 8, hf)), ALU.mult)
                    dve.tensor_tensor(dst_b[:, :, hf:DH], src[:, :, 0:hf], bcast(sin[:, :, hf:DH], (P, 8, hf)), ALU.mult).then_inc(rot_ready.sem, 1)
                    dve.wait_ge(sq_ready.sem, sq_ready.at(u, c + 1))
                    dve.tensor_reduce(v.ss[:, 8 * c:8 * c + 8], v.sq[:].rearrange("p (h d) -> p h d", h=8), AX.X, ALU.add).then_inc(ss_ready.sem, 1)
                if kind == "N":
                    y, z, rn = v.nt[:, 0, :], v.nt[:, 1, :], v.rn[:, t % 2, :]
                    n = [0]
                    def then(ins):
                        ins.then_inc(newton.sem, 1)
                        n[0] += 1
                        dve.wait_ge(newton.sem, newton.at(u, n[0]))
                    dve.wait_ge(ss_ready.sem, ss_ready.at(u, 4))
                    then(dve.tensor_scalar(v.ss[:], v.ss[:], 1e-24, None, ALU.max))
                    then(dve.tensor_scalar(z.bitcast(I32), v.ss[:].bitcast(I32), 1, None, ALU.arith_shift_right))
                    then(dve.tensor_scalar(y.bitcast(I32), z.bitcast(I32), -1.0, MAGIC, ALU.mult, ALU.add))
                    for _ in range(NEWTON):
                        then(dve.tensor_tensor(z, y, y, ALU.mult))
                        then(dve.scalar_tensor_tensor(z, z, -0.5, v.ss[:], ALU.mult, ALU.mult))
                        then(dve.scalar_tensor_tensor(y, z, 1.5, y, ALU.add, ALU.mult))
                    dve.wait_ge(p_ready.sem, p_ready.at(u - 2, 4))
                    yg, rg = y.rearrange("p (g n) -> p g n", g=2), rn.rearrange("p (g n) -> p g n", g=2)
                    dve.tensor_copy(rg[:, :, 8:16], yg[:, :, 8:16]).then_inc(rn_ready.sem, 1)
                    dve.tensor_scalar(rg[:, :, 0:8], yg[:, :, 0:8], 8.0, None, ALU.mult).then_inc(rn_ready.sem, 1)
                if kind == "S":
                    dve.wait_ge(s_full.sem, s_full.at(u, c + 1))
                    dve.wait_ge(rn_ready.sem, rn_ready.at(u, 2))
                    own = slice(16 * (c // 2) + c % 2, 16 * (c // 2) + 8, 2)
                    dve.tensor_reduce(v.mx[:, c % 2, :], sc[:, slot, :].rearrange("p (h j) -> p h j", h=4), AX.X, ALU.max).then_inc(mx_ready.sem, 1)
                    dve.wait_ge(mx_ready.sem, mx_ready.at(u, c + 1))
                    dve.wait_ge(p_ready.sem, p_ready.at(u, c - 1))
                    dve.scalar_tensor_tensor(v.nb[:, c % 2, :], v.mx[:, c % 2, :], -1.0, v.rn[:, t % 2, own], ALU.mult, ALU.mult).then_inc(nb_ready.sem, 1)
                if kind == "V":
                    dve.wait_ge(pT_full.sem, pT_full.at(u, c + 1))
                    dve.wait_ge(av_full.sem, av_full.at(u, c - 1))
                    dve.tensor_copy(v.pT[:, c % 2, :], tr[slot][:]).then_inc(pT_ready.sem, 1)
                if kind == "O":
                    dve.wait_ge(p_ready.sem, p_ready.at(u, 2 * c + 2))
                    dve.reciprocal(v.rs[:, c, :], v.psums[:, t % 2, 8 * c:8 * c + 8]).then_inc(rs_ready.sem, 1)
                    dve.wait_ge(rs_ready.sem, rs_ready.at(u, c + 1))
                    dve.wait_ge(av_full.sem, av_full.at(u, 2 * c + 2))
                    dve.wait_ge(oT_full.sem, oT_full.at(u - 1, c + 1))
                    dve.tensor_tensor(v.on[:, c, :].rearrange("p (h d) -> p h d", h=8), av[:].rearrange("p (h d) -> p h d", h=8),
                                      bcast(v.rs[:, c, :].unsqueeze(2), (P, 8, DH)), ALU.mult).then_inc(on_ready.sem, 1)
                if kind == "W":
                    dve.wait_ge(f_full.sem, f_full.at(u, f_count(step)))
                    xr = xrow(c, row(i, step))
                    dve.tensor_tensor(xr, xr, pj[slot][:], ALU.add).then_inc(xa_ready.sem, 1)
                if kind == "M":
                    dve.wait_ge(f_full.sem, f_full.at(u, f_count(step)))
                    dve.wait_ge(xa_ready.sem, xa_ready.at(u, 2))
                    for k in range(KC):
                        dve.tensor_tensor(v.xc[:, k, :], xrow(k, row(i, step), 1 - k), pj[slot][:], ALU.subtract).then_inc(xc_ready.sem, 1)
                if kind == "R":
                    dve.wait_ge(std_ready.sem, std_ready.at(u, 1))
                    dve.reciprocal(v.std, v.std).then_inc(rstd_ready.sem, 1)
                    dve.wait_ge(rstd_ready.sem, rstd_ready.at(u, 1))
                    dve.tensor_tensor(v.xc[:], v.xc[:], bcast(v.std.unsqueeze(1), (P, KC, S)), ALU.mult).then_inc(xm_ready.sem, 1)
                    dve.wait_ge(xm_ready.sem, xm_ready.at(u, 1))
                    for k in range(KC):
                        dve.tensor_scalar(v.xc[:, k, :], v.xc[:, k, :], v.lng[:, k:k + 1], v.lnb[:, k:k + 1], ALU.mult, ALU.add).then_inc(xn_ready.sem, 1)
                if kind == "U":
                    n = P if c < HC - 1 else LAST
                    dve.wait_ge(f_full.sem, f_full.at(u, f_count(step)))
                    dve.wait_ge(gate_ready.sem, gate_ready.at(u, c + 1))
                    dve.scalar_tensor_tensor(v.hid[0:n, c, :], pj[slot][0:n, :], v.b1c[0:n, c:c + 1], v.gate[0:n, c % 2, :],
                                             ALU.add, ALU.mult).then_inc(hid_ready.sem, 1)
                if kind == "Y":
                    dve.wait_ge(f_full.sem, f_full.at(u, f_count(step)))
                    xr = xrow(c, row(i, step))
                    dve.scalar_tensor_tensor(xr, pj[slot][:], v.b2c[:, c:c + 1], xr, ALU.add, ALU.add).then_inc(x_ready.sem, 1)
            run(dve, "dve", do)


def final(nc, a, sig, v):
    kept, summed, stored = sig("z_kept"), sig("z_sum"), sig("z_stored")
    bufs = [v.ffw[:, n * B * S:(n + 1) * B * S].rearrange("p (b s) -> p b s", b=B) for n in range(KC)]
    with nc.Block() as block:
        @block.sync
        def _(sp):
            for k in range(KC):
                sp.dma_start(bufs[k], a["kept"][:, k, :, :]).then_inc(kept.sem, 16)
                sp.wait_ge(kept.sem, 16 * (k + 1))
            for k in range(KC):
                sp.wait_ge(summed.sem, k + 1)
                sp.dma_start(a["out"][:, k, :, :], bufs[k]).then_inc(stored.sem, 16)
            sp.wait_ge(stored.sem, 16 * KC)

        @block.vector
        def _(dve):
            for k in range(KC):
                dve.wait_ge(kept.sem, 16 * (k + 1))
                dve.scalar_tensor_tensor(bufs[k], v.x[:, k, :, 1:ROW], v.tanhs[:, 1:2], bufs[k], ALU.mult, ALU.add).then_inc(summed.sem, 1)


def constants():
    f = np.float32
    half = np.arange(0, DH, 2, dtype=f)
    inv_freq = (f(1.0) / f(10000.0) ** (half / f(DH))).astype(f)
    tok = np.arange(S, dtype=f)
    freqs = tok[:, None] * inv_freq[None, :]
    base = ((half + f(0.4 * DH)) / f(1.4 * DH)).astype(f)
    power = ((tok - S // 2) / (W // 2)).astype(f)
    scale = base[None, :] ** power[:, None]
    cos, sin = np.cos(freqs), np.sin(freqs)
    inv = f(1.0) / scale
    rot = np.concatenate([cos * scale, cos * scale, -sin * scale, sin * scale,
                          cos * inv, cos * inv, -sin * inv, sin * inv], -1).astype(f)
    rotary = np.ascontiguousarray(rot.reshape(TILES, P, 4 * DH).transpose(1, 0, 2))
    mask = np.zeros((P, 2, P), f)
    i = np.arange(W)[:, None]
    j = np.arange(W)[None, :]
    causal, band = np.where(j <= i, 0.0, MASKED), np.where(j >= i, 0.0, MASKED)
    for first in range(2):
        mask[0:W, first, 0:W] = causal
        mask[0:W, first, W:P] = MASKED if first == 0 else band
        mask[W:P, first, 0:W] = band
        mask[W:P, first, W:P] = causal
    block = np.zeros((P, 8), f)
    block[np.arange(P), np.arange(P) // XD] = 1.0
    return {"rotary": rotary, "mask": mask, "bmask": block, "ident": np.eye(P, dtype=f),
            "mean_w": np.full((P, P), 1.0 / D, f)}


def lay_out(inp):
    g = {k: np.asarray(x) for k, x in inp.items()}

    def chunks(m):
        return np.ascontiguousarray(m.reshape(KC, P, -1).transpose(1, 0, 2))

    def column(x):
        return x.reshape(KC, P).T
    out = dict(constants())
    out["xT"] = chunks(g["x"].transpose(2, 0, 1).reshape(D, B * S)).reshape(P, KC, B, S)
    out["ctxT"] = chunks(g["ctx_1024"].transpose(2, 0, 1).reshape(D, B * CTX)).reshape(P, KC, B, CTX)
    out["g_xattn"], out["g_ffn"] = g["g_xattn"].reshape(1), g["g_ffn"].reshape(1)
    for name, w in (("Wq", "Wq"), ("Wk", "Wk"), ("Wv", "Wv"), ("Wo_x", "Wo")):
        out[name] = chunks(g["L0_xattn_" + w].T)
    out["cols"] = np.ascontiguousarray(np.concatenate([column(g["L0_xattn_" + n]) for n in ("bq", "bk", "bo")], 1))
    out["bv"] = g["L0_xattn_bv"]
    out["mlp"] = np.ascontiguousarray(np.concatenate([g["L0_xattn_w1"], g["L0_xattn_b1"][:, None], g["L0_xattn_w2"].T, np.zeros((CTX, P - CTX), np.float32), g["L0_xattn_b2"][:, None]], 1))
    out["w3"], out["b3"] = np.ascontiguousarray(g["L0_xattn_w3"].T), g["L0_xattn_b3"]
    qs, ks = g["L0_ffn_q_scale"], g["L0_ffn_k_scale"]
    swap = lambda s: np.concatenate([s[:, DH // 2:], s[:, :DH // 2]], 1)
    out["qk_scale"] = np.ascontiguousarray(np.concatenate([qs, swap(qs), ks, swap(ks)], 1))
    out["Wqkv"], out["Wo"], out["W1"], out["W2"] = (g["L0_ffn_" + n] for n in ("Wqkv", "Wo", "W1", "W2"))
    b1 = np.zeros((DEPTH, 2, HC * P), np.float32)
    b1[:, :, :HID] = g["L0_ffn_b1"].reshape(DEPTH, 2, HID)
    b1 = b1.reshape(DEPTH, 2 * HC, P).transpose(0, 2, 1)
    rest = [g["L0_ffn_" + n].reshape(DEPTH, KC, P).transpose(0, 2, 1) for n in ("b2", "ln_g", "ln_b")]
    out["small"] = np.ascontiguousarray(np.concatenate([b1] + rest, 2))
    return out


def kernel(**inputs):
    import concourse.bacc as bacc
    from concourse.bass_utils import run_bass_kernel_spmd

    nc = bacc.Bacc("TRN2", target_bir_lowering=False, num_devices=1)
    arrays = lay_out(inputs)
    a = {n: nc.dram_tensor("in_" + n, x.shape, F32, kind="ExternalInput").ap() for n, x in arrays.items()}
    a["kept"] = nc.dram_tensor("kept", (P, KC, B, S), F32, kind="Internal").ap()
    a["parts"] = nc.dram_tensor("parts", (DEPTH, CHUNKS, P, 2 * KC * 512), F32, kind="Internal").ap()
    a["out"] = nc.dram_tensor("out_stream", (P, KC, B, S), F32, kind="ExternalOutput").ap()
    build(nc, a)
    r = run_bass_kernel_spmd(nc, [{"in_" + n: np.ascontiguousarray(x) for n, x in arrays.items()}], core_ids=[0])
    y = r.results[0]["out_stream"]
    return np.ascontiguousarray(y.transpose(2, 3, 1, 0).reshape(B, S, D))
```

```python
from contextlib import ExitStack

import numpy as np

import concourse.bass as bass
from concourse import mybir

F32 = mybir.dt.float32
F32R = mybir.dt.float32r
BF16 = mybir.dt.bfloat16
I32 = mybir.dt.int32
ALU = mybir.AluOpType
ACT = mybir.ActivationFunctionType
AX = mybir.AxisListType

P = 128
B, S, D = 4, 512, 256
CTX = 64
XH, XD = 16, 16
KC = D // P
TILES = S // P
DEPTH, H, DH, W = 6, 16, 64, 64
INNER = H * DH
PAIRS = H // 2
HID = int(D * 4 * 2 / 3)
HC = -(-HID // P)
LAST = HID - (HC - 1) * P
ROW = S + 1
ITERS = DEPTH * B
COLUMN = (0, INNER, 512, INNER + 512, 2 * INNER, 2 * INNER + 512)
CHUNKS = len(COLUMN)
MASKED = -1.0e30
FFN_LOADS = 6
EXP_AND_LN = "natural_log_exp_and_others"


class Signal:

    def __init__(self, sem, per, credit=0):
        self.sem, self.per, self.credit = sem, per, credit

    def at(self, unit, n):
        value = unit * self.per + (n + self.credit)
        assert not isinstance(value, int) or value > 0
        return value


class Buffers:
    pass


def bcast(ap, shape):
    return ap.to_broadcast(list(shape))


def build(nc, a):
    with ExitStack() as ctx:
        def sb(name, shape, dt=F32):
            return ctx.enter_context(nc.sbuf_tensor(name, list(shape), dt))

        def sig(name, per=1, credit=0):
            return Signal(ctx.enter_context(nc.semaphore(name)), per, credit)

        v = Buffers()
        bank = {n: ctx.enter_context(nc.psum_tensor(n, [P, 512], F32)) for n in ("pj0", "pj1", "pj2", "tr0", "tr1", "av")}
        v.sc = ctx.enter_context(nc.psum_tensor("sc", [P, 2, 512], F32))
        v.pj = [bank["pj0"], bank["pj1"], bank["pj2"]]
        v.tr = [bank["tr0"], bank["tr1"]]
        v.av = bank["av"]

        v.x = sb("x", [P, KC, B, ROW])
        v.mean_w = sb("mean_w", [P, P])
        v.ident = sb("ident", [P, P])
        v.ident16 = sb("ident16", [P, P], BF16)
        v.mask16 = sb("mask16", [P, 2, P], BF16)
        v.eps = sb("eps", [P, 1])
        v.ln8 = sb("ln8", [P, 1])
        v.gates = sb("gates", [P, 2])
        v.tanhs = sb("tanhs", [P, 2])
        v.wqkv = sb("wqkv", [P, CHUNKS, 2, KC, 512], F32R)
        v.ffw = sb("ffw", [P, KC * 2 * HID + PAIRS * D + HC * D])
        v.w1 = v.ffw[:, 0:KC * 2 * HID].rearrange("p (k n) -> p k n", k=KC)
        v.wo = v.ffw[:, KC * 2 * HID:KC * 2 * HID + PAIRS * D].rearrange("p (m n) -> p m n", m=PAIRS)
        v.w2 = v.ffw[:, KC * 2 * HID + PAIRS * D:].rearrange("p (c n) -> p c n", c=HC)
        v.small = sb("small", [P, 2 * HC + 3 * KC])
        v.b1c, v.b2c = v.small[:, 0:2 * HC], v.small[:, 2 * HC:2 * HC + KC]
        v.lng, v.lnb = v.small[:, 2 * HC + KC:2 * HC + 2 * KC], v.small[:, 2 * HC + 2 * KC:]
        v.qk_scale = sb("qk_scale", [P, 4 * DH])
        v.rotary = sb("rotary", [P, TILES, 4 * DH])
        v.table = sb("table", [P, TILES, 4 * DH])
        v.xs = sb("xs", [P, 2, 2, KC, P], F32R)
        v.sq = sb("sq", [P, 512])
        v.raw = sb("raw", [P, 2, 512])
        v.rot_b = sb("rot_b", [P, 2, 512])
        v.qk = sb("qk", [P, 4, 512])
        v.ss = sb("ss", [P, 32])
        v.ln_ss = sb("ln_ss", [P, 32])
        v.rn = sb("rn", [P, 2, 32])
        v.qT = sb("qT", [P, PAIRS, P])
        v.kT = sb("kT", [P, 2, PAIRS, P])
        v.v_even = sb("v_even", [P, TILES, INNER])
        v.v_odd = sb("v_odd", [P, 2, INNER])
        v.mx = sb("mx", [P, 2, 4])
        v.nb = sb("nb", [P, 2, 4])
        v.probs = sb("probs", [P, 2, 512])
        v.psums = sb("psums", [P, 2, H])
        v.rs = sb("rs", [P, 2, 8])
        v.pT = sb("pT", [P, 2, 512])
        v.on = sb("on", [P, 2, 512])
        v.oT = sb("oT", [P, PAIRS, S])
        v.kept = [v.oT[:].rearrange("p m s -> p (m s)")[:, k * B * S:(k + 1) * B * S].rearrange("p (b s) -> p b s", b=B) for k in range(KC)]
        v.xc = sb("xc", [P, KC, S])
        v.gate = sb("gate", [P, 2, S])
        v.std = v.gate[:, 0, :]
        v.mask = v.gate[:, 1, 0:2 * P].rearrange("p (n j) -> p n j", n=2)
        v.hid = sb("hid", [P, HC, S])
        v.sqf = v.hid[:, 0:2, :]

        v.wx = v.ffw[:, 0:3968]
        v.whole = [v.ffw[:, 3968 + n * KC * 512:3968 + (n + 1) * KC * 512].rearrange("p (k n) -> p k n", k=KC) for n in range(2)]
        v.xw = [v.wx[:, n * KC * D:(n + 1) * KC * D].rearrange("p (k n) -> p k n", k=KC) for n in range(4)]
        v.ctxT = v.wx[:, 2048:2048 + KC * B * CTX].rearrange("p (k b c) -> p k b c", k=KC, b=B)
        v.ctx_b = v.wx[:, 2560:2560 + KC * 2 * CTX].rearrange("p (k e c) -> p k e c", k=KC, e=2)
        v.bv_row = v.wx[:, 2816:2816 + D]
        v.cols = v.wx[:, 3072:3072 + 3 * KC]
        v.bmask = v.wx[:, 3080:3088]
        v.mlp = v.wx[0:CTX, 3832:3832 + 133]
        v.w3_col, v.b3_col = v.wx[0:CTX, 3160:3161], v.wx[:, 3161:3162]
        v.w1s = v.wx[0:CTX, 3162:3165]
        v.w3w = v.wx[0:CTX, 3168:3168 + P]
        v.h1 = v.wx[0:CTX, 3300:3300 + XH]
        v.h2 = v.wx[0:CTX, 3320:3320 + XH]
        v.temp = v.wx[:, 3340:3340 + XH]
        v.feats = v.wx[:, 3360:3360 + TILES * 3 * XH].rearrange("p (t f h) -> p t f h", t=TILES, f=3)
        v.sums = [v.wx[:, o:o + 4 * XH].rearrange("p (n h) -> p n h", n=4) for o in (3600, 3092)]
        v.ksum = v.wx[:, 3664:3664 + KC]
        v.ksbd = v.wx[:, 3668:3668 + KC * 8].rearrange("p (m h) -> p m h", m=KC)
        v.xqT = v.qT[:, 0:8, :].rearrange("p a b -> p (a b)").rearrange("p (m s) -> p m s", m=KC)
        v.xkT = v.wx[:, 3700:3700 + KC * CTX].rearrange("p (m c) -> p m c", m=KC)
        v.kbd = v.kT[:, 0, :, :].rearrange("p a b -> p (a b)").rearrange("p (m h c) -> p m h c", m=KC, h=8)
        v.vbd = v.pT[:, :, :].rearrange("p a b -> p (a b)").rearrange("p (r n) -> p r n", r=8)
        v.dm = v.oT[:, :, :].rearrange("p a b -> p (a b)").rearrange("p (t h c) -> p t h c", t=TILES, h=XH)
        def two(u, w):
            return [z.rearrange("p a b -> p (a b)").rearrange("p (h c) -> p h c", h=XH) for z in (u, w)]
        v.ex, v.ey, v.at = two(v.probs[:], v.raw[:]), two(v.qk[:, 0:2, :], v.rot_b[:]), two(v.on[:], v.qk[:, 2:4, :])
        v.atT = v.v_even[:, :, :].rearrange("p a b -> p (a b)").rearrange("p (r s) -> p r s", r=8)
        v.xoT = v.hid[:, 2:4, :]
        v.ytmp = v.hid[:, 4:6, :]

        cross_attention(nc, a, sig, v)
        norm_between(nc, a, sig, v)
        stack(nc, a, sig, v)
        final(nc, a, sig, v)




def cross_attention(nc, a, sig, v):
    x, pj, tr, av, sc = v.x, v.pj, v.tr, v.av, v.sc
    loaded = sig("a_loaded")
    setup = sig("a_setup")
    mean_ready, xc_ready, sq_ready, var_ready = sig("a_mean"), sig("a_xc", 2), sig("a_sq"), sig("a_var")
    std_ready, rstd_ready, xn_ready = sig("a_std"), sig("a_rstd"), sig("a_xn")
    ctx_ready, k_full, k_ready, kbd_ready = sig("a_ctx"), sig("a_kfull"), sig("a_k", 2), sig("a_kbd", 2)
    v_full, vbd_ready = sig("a_vfull"), sig("a_vbd", 4)
    q_full, q_ready = sig("a_qfull", 2), sig("a_q", 2)
    s_full, max_ready, dm_ready = sig("a_sfull", TILES), sig("a_max", TILES), sig("a_dm", TILES)
    ksum_ready, m_full, m_ready = sig("a_ksum", 1 + KC), sig("a_mfull"), sig("a_m")
    e_ready, esum_ready, em_ready, e2_ready = sig("a_e", TILES), sig("a_esum", 2 * TILES), sig("a_em", TILES), sig("a_e2", TILES)
    f_step, f_ready, f_full = sig("a_fstep", 2 * TILES), sig("a_f", TILES), sig("a_ffull")
    h_step, h1_in, h1_ready, h2_full, h2_ready = sig("a_hstep", 2), sig("a_h1in"), sig("a_h1"), sig("a_h2full"), sig("a_h2")
    t_full, t_step, t_in, t_ready, t_half = sig("a_tfull"), sig("a_tstep"), sig("a_tin"), sig("a_t"), sig("a_thalf")
    ds_ready, p_ready, r_step, at_ready = sig("a_ds", TILES), sig("a_p", TILES), sig("a_rstep", 3 * TILES), sig("a_at", TILES)
    at_full, atT_ready = sig("a_atfull", TILES), sig("a_atT", 2 * TILES)
    o_full, o_ready, y_full, y_step, x_ready = sig("a_ofull", 2), sig("a_o", 2), sig("a_yfull", 2), sig("a_ystep", 2), sig("a_x", 2)
    kept = sig("a_kept", 16 * KC)
    whole_in = [sig("a_whole%d" % n, CHUNKS // 2 * 16) for n in range(2)]
    part_step, parts_ready = sig("a_partstep", 2 * CHUNKS), sig("a_parts", CHUNKS)
    parts_out = [sig("a_partsout%d" % c, 16) for c in range(CHUNKS)]
    loads = [
        (x[:, :, :, 1:ROW], a["xT"]), (v.mean_w[:], a["mean_w"]), (v.ident[:], a["ident"]), (v.mask, a["mask"]),
        (v.ctxT, a["ctxT"]), (v.bmask, a["bmask"]), (v.cols, a["cols"]), (v.mlp, a["mlp"]),
        (v.w3_col, a["w3"]), (v.rotary[:], a["rotary"]),
        (v.xw[0], a["Wq"]), (v.xw[1], a["Wk"]), (v.xw[2], a["Wv"]), (v.xw[3], a["Wo_x"]),
        (v.gates[:, 0:1], a["g_xattn"].partition_broadcast(P)), (v.gates[:, 1:2], a["g_ffn"].partition_broadcast(P)),
        (v.bv_row, a["bv"].partition_broadcast(P)), (v.b3_col, a["b3"].partition_broadcast(P)),
        (v.qk_scale[:], a["qk_scale"][0:1, :].rearrange("l n -> (l n)").partition_broadcast(P)),
    ]

    def all_loaded(eng):
        eng.wait_ge(loaded.sem, 16 * (len(loads) + 1))

    with nc.Block() as block:
        @block.sync
        def _(sp):
            for k in range(KC):
                sp.dma_start(x[:, k, :, 1:ROW], a["xT"][:, k, :, :]).then_inc(loaded.sem, 16)
            for dst, src in loads[1:]:
                sp.dma_start(dst, src).then_inc(loaded.sem, 16)
            all_loaded(sp)

            def load_whole(layer, c):
                sp.dma_start(v.whole[c % 2], a["Wqkv"][bass.ds(layer, 1), :, COLUMN[c]:COLUMN[c] + 512]
                             .rearrange("l (k p) n -> p (l k) n", p=P)).then_inc(whole_in[c % 2].sem, 16)
            def parts_to_dram(n, c):
                sp.wait_ge(parts_ready.sem, parts_ready.at(n - 1, c + 1))
                sp.dma_start(a["parts"][bass.ds(n, 1), c].rearrange("l p n -> p (l n)"),
                             v.wqkv[:, c].rearrange("p a k n -> p (a k n)").bitcast(F32)).then_inc(parts_out[c].sem, 16)
            load_whole(1, 0)
            load_whole(1, 1)
            with sp.Fori(1, DEPTH - 1) as n:
                for c in range(CHUNKS):
                    parts_to_dram(n, c)
                    load_whole(n + (c + 2) // CHUNKS, (c + 2) % CHUNKS)
            for c in range(CHUNKS):
                parts_to_dram(DEPTH - 1, c)
                load_whole(0 if c + 2 >= CHUNKS else DEPTH - 1, (c + 2) % CHUNKS)
            for c in range(CHUNKS - 2):
                sp.wait_ge(parts_ready.sem, parts_ready.at(DEPTH - 1, c + 1))
                load_whole(0, c + 2)
            with sp.Fori(0, B) as b:
                sp.wait_ge(x_ready.sem, x_ready.at(b, 2))
                for k in range(KC):
                    sp.dma_start(a["kept"][:, k, bass.ds(b, 1), :].rearrange("p b s -> p (b s)"),
                                 x[:, k, bass.ds(b, 1), 1:ROW].rearrange("p b s -> p (b s)")).then_inc(kept.sem, 16)
            for c in range(CHUNKS):
                sp.wait_ge(parts_out[c].sem, parts_out[c].at(DEPTH - 1, 0))
            sp.wait_ge(kept.sem, kept.at(B, 0))

        @block.gpsimd
        def _(pool):
            pool.memset(x[:, :, :, 0:1], 0.0)
            pool.memset(v.eps[:], 1e-5)
            pool.memset(v.ln8[:], float(np.log(8.0)))
            pool.memset(v.vbd, 0.0)
            pool.memset(v.v_even[:, 0, 0:1], 0.0)
            pool.drain().then_inc(setup.sem, 1)

            def split(n, c, first):
                pool.wait_ge(whole_in[c % 2].sem, whole_in[c % 2].at(n, 16 * (c // 2 + 1)))
                if not first:
                    pool.wait_ge(parts_out[c].sem, parts_out[c].at(n, 0))
                high, low = v.wqkv[:, c, 0], v.wqkv[:, c, 1]
                pool.nop().then_inc(part_step.sem, 1)
                pool.tensor_copy(high, v.whole[c % 2]).then_inc(part_step.sem, 1)
                pool.wait_ge(part_step.sem, part_step.at(n, 2 * c + 2))
                pool.tensor_tensor(low, v.whole[c % 2], high, ALU.subtract).then_inc(parts_ready.sem, 1)
            for c in range(CHUNKS):
                split(0, c, True)
            with pool.Fori(1, DEPTH) as n:
                for c in range(CHUNKS):
                    split(n, c, False)

        @block.tensor
        def _(pe):
            all_loaded(pe)
            pe.wait_ge(setup.sem, setup.at(0, 1))
            with pe.Fori(0, B) as b:
                def xrow(k):
                    return x[:, k, bass.ds(b, 1), 1:ROW].rearrange("p b s -> p (b s)")
                for k in range(KC):
                    mm = pe.matmul(pj[0][:], v.mean_w[:], xrow(k), start=(k == 0), stop=(k == KC - 1))
                mm.then_inc(mean_ready.sem, 1)
                for m in range(KC):
                    for k in range(KC):
                        mm = pe.matmul(pj[2][:, m * CTX:(m + 1) * CTX], v.xw[1][:, k, m * P:(m + 1) * P],
                                       v.ctxT[:, k, bass.ds(b, 1), :].rearrange("p b c -> p (b c)"),
                                       start=(k == 0), stop=(k == KC - 1))
                mm.then_inc(k_full.sem, 1)
                pe.wait_ge(ctx_ready.sem, ctx_ready.at(b, 1))
                for k in range(KC):
                    mm = pe.matmul(tr[0][:, 0:D], v.ctx_b[:, k, :, :].rearrange("p e c -> p (e c)"), v.xw[2][:, k, :],
                                   start=(k == 0), stop=(k == KC - 1))
                mm.then_inc(v_full.sem, 1)
                pe.wait_ge(sq_ready.sem, sq_ready.at(b, 1))
                for k in range(KC):
                    mm = pe.matmul(pj[1][:], v.mean_w[:], v.sqf[:, k, :], start=(k == 0), stop=(k == KC - 1))
                mm.then_inc(var_ready.sem, 1)
                pe.wait_ge(xn_ready.sem, xn_ready.at(b, 1))
                for m in range(KC):
                    for k in range(KC):
                        mm = pe.matmul(pj[m][:], v.xw[0][:, k, m * P:(m + 1) * P], v.xc[:, k, :],
                                       start=(k == 0), stop=(k == KC - 1))
                    mm.then_inc(q_full.sem, 1)
                pe.wait_ge(q_ready.sem, q_ready.at(b, 2))
                pe.wait_ge(kbd_ready.sem, kbd_ready.at(b, 2))
                pe.wait_ge(ksum_ready.sem, ksum_ready.at(b, 1 + KC))
                for t in range(TILES):
                    for m in range(KC):
                        o = (KC * t + m) * 8
                        mm = pe.matmul(pj[2][:, 256 + o:256 + o + 8], v.xqT[:, m, t * P:(t + 1) * P], v.ksbd[:, m, :], start=True, stop=True)
                mm.then_inc(m_full.sem, 1)
                for t in range(TILES):
                    if t > 0:
                        pe.wait_ge(dm_ready.sem, dm_ready.at(b, t))
                    for m in range(KC):
                        mm = pe.matmul(sc[:, m, :], v.xqT[:, m, t * P:(t + 1) * P],
                                       v.kbd[:, m, :, :].rearrange("p h c -> p (h c)"), start=True, stop=True)
                    mm.then_inc(s_full.sem, 1)
                pe.wait_ge(m_ready.sem, m_ready.at(b, 1))
                for t in range(TILES):
                    pe.wait_ge(f_ready.sem, f_ready.at(b, t + 1))
                    mm = pe.matmul(tr[1][:, 0:3 * XH], v.mean_w[:], v.feats[:, t, :, :].rearrange("p f h -> p (f h)"),
                                   start=(t == 0), stop=(t == TILES - 1))
                mm.then_inc(f_full.sem, 1)
                pe.wait_ge(h1_ready.sem, h1_ready.at(b, 1))
                pe.matmul(tr[1][:, 64:64 + XH], v.mlp[:, 4:4 + P], v.h1, start=True, stop=True).then_inc(h2_full.sem, 1)
                pe.wait_ge(h2_ready.sem, h2_ready.at(b, 1))
                pe.matmul(tr[1][:, 128:128 + XH], v.w3w, v.h2, start=True, stop=True).then_inc(t_full.sem, 1)
                for t in range(TILES):
                    pe.wait_ge(at_ready.sem, at_ready.at(b, t + 1))
                    if t > 1:
                        pe.wait_ge(atT_ready.sem, atT_ready.at(b, 2 * (t - 1)))
                    for r in range(8):
                        mm = pe.transpose((tr, pj)[t % 2][r // 4][:, (r % 4) * P:(r % 4 + 1) * P],
                                          v.at[t % 2][:, 2 * r:2 * r + 2, :].rearrange("p h c -> p (h c)"), v.ident[:])
                    mm.then_inc(at_full.sem, 1)
                pe.wait_ge(atT_ready.sem, atT_ready.at(b, 2 * TILES))
                pe.wait_ge(vbd_ready.sem, vbd_ready.at(b, 4))
                for m in range(KC):
                    for r in range(4):
                        mm = pe.matmul(pj[m][:], v.vbd[:, 4 * m + r, :], v.atT[:, 4 * m + r, :], start=(r == 0), stop=(r == 3))
                    mm.then_inc(o_full.sem, 1)
                pe.wait_ge(o_ready.sem, o_ready.at(b, 2))
                for m in range(KC):
                    for k in range(KC):
                        mm = pe.matmul(sc[:, m, :], v.xw[3][:, k, m * P:(m + 1) * P], v.xoT[:, k, :],
                                       start=(k == 0), stop=(k == KC - 1))
                    mm.then_inc(y_full.sem, 1)

        @block.scalar
        def _(act):
            all_loaded(act)
            act.wait_ge(setup.sem, setup.at(0, 1))
            act.activation(v.tanhs[:], v.gates[:], ACT.Tanh).then_inc(setup.sem, 1)
            act.preload_act_table_set(EXP_AND_LN)
            with act.Fori(0, B) as b:
                act.wait_ge(k_full.sem, k_full.at(b, 1))
                for m in range(KC):
                    act.activation(v.xkT[:, m, :], pj[2][:, m * CTX:(m + 1) * CTX], ACT.Identity,
                                   bias=v.cols[:, KC + m:KC + m + 1]).then_inc(k_ready.sem, 1)
                act.wait_ge(xc_ready.sem, xc_ready.at(b, 2))
                act.activation(v.sqf, v.xc[:], ACT.Square).then_inc(sq_ready.sem, 1)
                act.wait_ge(var_ready.sem, var_ready.at(b, 1))
                act.activation(v.std, pj[1][:], ACT.Ln, bias=v.eps[:]).then_inc(std_ready.sem, 1)
                act.wait_ge(std_ready.sem, std_ready.at(b, 1))
                act.activation(v.std, v.std, ACT.Exp, scale=-0.5).then_inc(rstd_ready.sem, 1)
                for m in range(KC):
                    act.wait_ge(q_full.sem, q_full.at(b, m + 1))
                    act.activation(v.xqT[:, m, :], pj[m][:], ACT.Identity, bias=v.cols[:, m:m + 1]).then_inc(q_ready.sem, 1)
                for t in range(TILES + 1):
                    if t < TILES:
                        act.wait_ge(dm_ready.sem, dm_ready.at(b, t + 1))
                        if t > 1:
                            act.wait_ge(e2_ready.sem, e2_ready.at(b, t - 1))
                        act.activation(v.ex[t % 2], v.dm[:, t, :, :], ACT.Exp, scale=XD ** -0.5).then_inc(e_ready.sem, 1)
                    if t > 0:
                        act.wait_ge(em_ready.sem, em_ready.at(b, t))
                        if t > 2:
                            act.wait_ge(f_ready.sem, f_ready.at(b, t - 2))
                        act.activation(v.ey[(t - 1) % 2], v.ex[(t - 1) % 2], ACT.Square).then_inc(e2_ready.sem, 1)
                act.wait_ge(h1_in.sem, h1_in.at(b, 1))
                act.activation(v.h1, v.h1, ACT.Gelu, bias=v.mlp[:, 3:4]).then_inc(h1_ready.sem, 1)
                act.wait_ge(h2_full.sem, h2_full.at(b, 1))
                act.activation(v.h2, tr[1][0:CTX, 64:64 + XH], ACT.Gelu, bias=v.mlp[:, 132:133]).then_inc(h2_ready.sem, 1)
                act.preload_act_table_set(EXP_AND_LN)
                act.wait_ge(t_in.sem, t_in.at(b, 1))
                act.activation(v.temp, v.temp, ACT.Exp, scale=-1.0).then_inc(t_ready.sem, 1)
                for t in range(TILES + 1):
                    if t < TILES:
                        act.wait_ge(ds_ready.sem, ds_ready.at(b, t + 1))
                        if t > 1:
                            act.wait_ge(at_ready.sem, at_ready.at(b, t - 1))
                        act.activation(v.ex[t % 2], v.dm[:, t, :, :], ACT.Exp).then_inc(p_ready.sem, 1)
                    if t > 0:
                        act.wait_ge(at_full.sem, at_full.at(b, t))
                        for n in range(2):
                            act.activation(v.atT[:, 4 * n:4 * n + 4, (t - 1) * P:t * P],
                                           (tr, pj)[(t - 1) % 2][n][:].rearrange("p (r q) -> p r q", r=4), ACT.Copy).then_inc(atT_ready.sem, 1)
                for m in range(KC):
                    act.wait_ge(o_full.sem, o_full.at(b, m + 1))
                    act.activation(v.xoT[:, m, :], pj[m][:], ACT.Copy).then_inc(o_ready.sem, 1)

        @block.vector
        def _(dve):
            all_loaded(dve)
            dve.wait_ge(setup.sem, setup.at(0, 2))
            for f, factor in enumerate((D * XD ** -0.5 / (S * CTX), D * XD ** -0.5 / S, D / (S * (CTX - 1.0)))):
                dve.tensor_scalar(v.w1s[:, f:f + 1], v.mlp[:, f:f + 1], factor, None, ALU.mult)
            dve.tensor_copy(v.w3w, bcast(v.w3_col, (CTX, P)))
            dve.tensor_copy(v.ident16[:], v.ident[:])
            dve.tensor_copy(v.mask16[:], v.mask).then_inc(setup.sem, 1)
            dve.wait_ge(setup.sem, setup.at(0, 3))
            with dve.Fori(0, B) as b:
                def xrow(k):
                    return x[:, k, bass.ds(b, 1), 1:ROW].rearrange("p b s -> p (b s)")
                dve.tensor_copy(v.ctx_b, bcast(v.ctxT[:, :, bass.ds(b, 1), :], (P, KC, 2, CTX))).then_inc(ctx_ready.sem, 1)
                dve.wait_ge(mean_ready.sem, mean_ready.at(b, 1))
                for k in range(KC):
                    dve.tensor_tensor(v.xc[:, k, :], xrow(k), pj[0][:], ALU.subtract).then_inc(xc_ready.sem, 1)
                dve.wait_ge(k_ready.sem, k_ready.at(b, 2))
                for m in range(KC):
                    dve.tensor_tensor(v.kbd[:, m, :, :], bcast(v.xkT[:, m:m + 1, :], (P, 8, CTX)),
                                      bcast(v.bmask.unsqueeze(2), (P, 8, CTX)), ALU.mult).then_inc(kbd_ready.sem, 1)
                dve.tensor_reduce(v.ksum, v.xkT, AX.X, ALU.add).then_inc(ksum_ready.sem, 1)
                dve.wait_ge(ksum_ready.sem, ksum_ready.at(b, 1))
                for m in range(KC):
                    dve.tensor_scalar(v.ksbd[:, m, :], v.bmask, v.ksum[:, m:m + 1], None, ALU.mult).then_inc(ksum_ready.sem, 1)
                dve.wait_ge(v_full.sem, v_full.at(b, 1))
                for m in range(KC):
                    for e in range(2):
                        rows = slice(e * CTX, (e + 1) * CTX)
                        src = tr[0][rows, m * P:(m + 1) * P].rearrange("p (r n) -> p r n", r=4)[:, :, e * XD:(e + 1) * XD]
                        row = v.bv_row[rows, m * P:(m + 1) * P].rearrange("p (r n) -> p r n", r=4)[:, :, e * XD:(e + 1) * XD]
                        dst = v.vbd[rows, 4 * m, e * XD:(e + 1) * XD]
                        dst = bass.AP(dst.tensor, dst.offset, [list(dst.ap[0]), [P + 2 * XD, 4], [1, XD]])
                        dve.tensor_tensor(dst, src, row, ALU.add).then_inc(vbd_ready.sem, 1)
                dve.wait_ge(rstd_ready.sem, rstd_ready.at(b, 1))
                dve.tensor_tensor(v.xc[:], v.xc[:], bcast(v.std.unsqueeze(1), (P, KC, S)), ALU.mult).then_inc(xn_ready.sem, 1)
                dve.wait_ge(m_full.sem, m_full.at(b, 1))
                dve.tensor_copy(v.feats[:, :, 0, :], pj[2][:, 256:256 + TILES * XH].rearrange("p (t h) -> p t h", t=TILES)).then_inc(m_ready.sem, 1)

                def scores_less_maximum(t):
                    dve.wait_ge(s_full.sem, s_full.at(b, t + 1))
                    s4 = sc[:, :, :].rearrange("p m (h c) -> p (m h) c", c=CTX)
                    dve.tensor_reduce(v.feats[:, t, 1, :], s4, AX.X, ALU.max).then_inc(max_ready.sem, 1)
                    dve.wait_ge(max_ready.sem, max_ready.at(b, t + 1))
                    dve.tensor_tensor(v.dm[:, t, :, :], s4, bcast(v.feats[:, t, 1, :].unsqueeze(2), (P, XH, CTX)),
                                      ALU.subtract).then_inc(dm_ready.sem, 1)

                def less_mean(t):
                    e, sums = v.ex[t % 2], v.sums[t % 2]
                    dve.wait_ge(e_ready.sem, e_ready.at(b, t + 1))
                    dve.tensor_reduce(sums[:, 0, :], e, AX.X, ALU.add).then_inc(esum_ready.sem, 1)
                    dve.wait_ge(esum_ready.sem, esum_ready.at(b, 2 * t + 1))
                    dve.tensor_scalar(sums[:, 1, :], sums[:, 0, :], 1.0 / CTX, None, ALU.mult)
                    dve.reciprocal(sums[:, 2, :], sums[:, 0, :]).then_inc(esum_ready.sem, 1)
                    dve.wait_ge(esum_ready.sem, esum_ready.at(b, 2 * t + 2))
                    dve.tensor_tensor(e, e, bcast(sums[:, 1, :].unsqueeze(2), (P, XH, CTX)), ALU.subtract).then_inc(em_ready.sem, 1)

                def variance(t):
                    sums = v.sums[t % 2]
                    dve.wait_ge(e2_ready.sem, e2_ready.at(b, t + 1))
                    dve.tensor_reduce(sums[:, 3, :], v.ey[t % 2], AX.X, ALU.add).then_inc(f_step.sem, 1)
                    dve.wait_ge(f_step.sem, f_step.at(b, 2 * t + 1))
                    dve.tensor_tensor(sums[:, 3, :], sums[:, 3, :], sums[:, 2, :], ALU.mult).then_inc(f_step.sem, 1)
                    dve.wait_ge(f_step.sem, f_step.at(b, 2 * t + 2))
                    dve.tensor_tensor(v.feats[:, t, 2, :], sums[:, 3, :], sums[:, 2, :], ALU.mult).then_inc(f_ready.sem, 1)
                for t in range(TILES + 2):
                    if t < TILES:
                        scores_less_maximum(t)
                    if 0 < t <= TILES:
                        less_mean(t - 1)
                    if t > 1:
                        variance(t - 2)
                dve.wait_ge(f_full.sem, f_full.at(b, 1))
                dve.tensor_scalar(v.h1, tr[1][0:CTX, 0:XH], v.w1s[:, 0:1], None, ALU.mult).then_inc(h_step.sem, 1)
                dve.wait_ge(h_step.sem, h_step.at(b, 1))
                dve.scalar_tensor_tensor(v.h1, tr[1][0:CTX, XH:2 * XH], v.w1s[:, 1:2], v.h1, ALU.mult, ALU.add).then_inc(h_step.sem, 1)
                dve.wait_ge(h_step.sem, h_step.at(b, 2))
                dve.scalar_tensor_tensor(v.h1, tr[1][0:CTX, 2 * XH:3 * XH], v.w1s[:, 2:3], v.h1, ALU.mult, ALU.add).then_inc(h1_in.sem, 1)
                dve.wait_ge(t_full.sem, t_full.at(b, 1))
                dve.tensor_scalar(v.temp, tr[1][:, 128:128 + XH], v.b3_col, float(np.float32(np.log(0.1))), ALU.add, ALU.max).then_inc(t_step.sem, 1)
                dve.wait_ge(t_step.sem, t_step.at(b, 1))
                dve.tensor_scalar(v.temp, v.temp, float(np.float32(np.log(10.0))), None, ALU.min).then_inc(t_in.sem, 1)
                dve.wait_ge(t_ready.sem, t_ready.at(b, 1))
                dve.tensor_scalar(v.temp, v.temp, 0.5, None, ALU.mult).then_inc(t_half.sem, 1)
                dve.wait_ge(t_half.sem, t_half.at(b, 1))
                for t in range(TILES + 1):
                    if t < TILES:
                        dve.tensor_tensor(v.dm[:, t, :, :], v.dm[:, t, :, :], bcast(v.temp.unsqueeze(2), (P, XH, CTX)), ALU.mult).then_inc(ds_ready.sem, 1)
                    if t == 0:
                        continue
                    u = t - 1
                    e, sums = v.ex[u % 2], v.sums[u % 2]
                    dve.wait_ge(p_ready.sem, p_ready.at(b, u + 1))
                    dve.tensor_reduce(sums[:, 0, :], e, AX.X, ALU.add).then_inc(r_step.sem, 1)
                    dve.wait_ge(r_step.sem, r_step.at(b, 3 * u + 1))
                    dve.reciprocal(sums[:, 1, :], sums[:, 0, :]).then_inc(r_step.sem, 1)
                    dve.wait_ge(r_step.sem, r_step.at(b, 3 * u + 2))
                    dve.tensor_scalar(sums[:, 2, :], sums[:, 1, :], 0.0, None, ALU.max).then_inc(r_step.sem, 1)
                    dve.wait_ge(r_step.sem, r_step.at(b, 3 * u + 3))
                    if u > 1:
                        dve.wait_ge(at_full.sem, at_full.at(b, u - 1))
                    dve.scalar_tensor_tensor(v.at[u % 2], e, 0.0, bcast(sums[:, 2, :].unsqueeze(2), (P, XH, CTX)),
                                             ALU.max, ALU.mult).then_inc(at_ready.sem, 1)
                for m in range(KC):
                    dve.wait_ge(y_full.sem, y_full.at(b, m + 1))
                    dve.tensor_scalar(v.ytmp[:, m, :], sc[:, m, :], v.cols[:, 2 * KC + m:2 * KC + m + 1], v.tanhs[:, 0:1],
                                      ALU.add, ALU.mult).then_inc(y_step.sem, 1)
                    dve.wait_ge(y_step.sem, y_step.at(b, m + 1))
                    dve.tensor_tensor(xrow(m), xrow(m), v.ytmp[:, m, :], ALU.add).then_inc(x_ready.sem, 1)


def norm_between(nc, a, sig, v):
    x = v.x
    means, variances = v.pj[0:2], (v.pj[2], v.tr[0])
    xc, sq = (v.xc[:], v.xoT), (v.sqf, v.ytmp)
    std = v.gate[:, 0, :], v.gate[:, 1, :]
    mean_ready, xc_ready, sq_ready, var_ready = sig("n_mean"), sig("n_xc", 2), sig("n_sq"), sig("n_var")
    std_ready, rstd_ready, x_ready, zero = sig("n_std"), sig("n_rstd"), sig("n_x", 2), sig("n_zero")
    with nc.Block() as block:
        @block.gpsimd
        def _(pool):
            pool.memset(v.v_even[:, 0, :], 0.0).then_inc(zero.sem, 1)

        @block.tensor
        def _(pe):
            with pe.Fori(0, B // 2) as n:
                for e in range(2):
                    for k in range(KC):
                        mm = pe.matmul(means[e][:], v.mean_w[:], x[:, k, bass.ds(2 * n + e, 1), 1:ROW].rearrange("p b s -> p (b s)"),
                                       start=(k == 0), stop=(k == KC - 1))
                    mm.then_inc(mean_ready.sem, 1)
                for e in range(2):
                    pe.wait_ge(sq_ready.sem, sq_ready.at(2 * n + e, 1))
                    for k in range(KC):
                        mm = pe.matmul(variances[e][:], v.mean_w[:], sq[e][:, k, :], start=(k == 0), stop=(k == KC - 1))
                    mm.then_inc(var_ready.sem, 1)

        @block.scalar
        def _(act):
            act.preload_act_table_set(EXP_AND_LN)
            with act.Fori(0, B // 2) as n:
                for e in range(2):
                    act.wait_ge(xc_ready.sem, xc_ready.at(2 * n + e, 2))
                    act.activation(sq[e], xc[e], ACT.Square).then_inc(sq_ready.sem, 1)
                for e in range(2):
                    act.wait_ge(var_ready.sem, var_ready.at(2 * n + e, 1))
                    act.activation(std[e], variances[e][:], ACT.Ln, bias=v.eps[:]).then_inc(std_ready.sem, 1)
                    act.wait_ge(std_ready.sem, std_ready.at(2 * n + e, 1))
                    act.activation(std[e], std[e], ACT.Exp, scale=-0.5).then_inc(rstd_ready.sem, 1)

        @block.vector
        def _(dve):
            with dve.Fori(0, B // 2) as n:
                def xrow(k, e):
                    return x[:, k, bass.ds(2 * n + e, 1), 1:ROW].rearrange("p b s -> p (b s)")
                for e in range(2):
                    dve.wait_ge(mean_ready.sem, mean_ready.at(2 * n + e, 1))
                    for k in range(KC):
                        dve.tensor_tensor(xc[e][:, k, :], xrow(k, e), means[e][:], ALU.subtract).then_inc(xc_ready.sem, 1)
                for e in range(2):
                    dve.wait_ge(rstd_ready.sem, rstd_ready.at(2 * n + e, 1))
                    for k in range(KC):
                        dve.tensor_tensor(xrow(k, e), xc[e][:, k, :], std[e], ALU.mult).then_inc(x_ready.sem, 1)
                dve.wait_ge(x_ready.sem, x_ready.at(2 * n + 2, 0))


ORDER = """
S00 V-13 P10 A-12 X-10 P11 P12 N10
S01 V00
S02 A-13 O-11 P13 P14 V01 A00 N11
S03 V02 A01 O00 X-11 T10 T11 W00 P15 T12 T13
S10 P20 V03 A02 X00 W01 P21
S11 P22 V10 A03 P23 N20
S12 P24 O01 M00 V11 A10 X01 N21
S13 V12 A11 O10 R00 T20 T21 P25 V13 A12 X10 T22 G00 T23 U00 G01 A13 O11 U01 G02 U02 G03 U03 G04 U04 G05 U05
S20 P30 P31
S21 P32 V20 Y00 P33 N30
S22 P34 V21 A20 X11 N31
S23 V22 A21 O20 T30 T31 P35 T32 T33
S30 V23 P40 A22 X20 P41
S31 P42 V30 A23 O21 P43 N40
S32 P44 Y01 V31 A30 X21 N41
S33 V32 A31 O30 T40 T41 P45 T42 T43
"""


def steps_of(first, ffn, following):
    steps = [(w[0], int(w[1:-1]), int(w[-1])) for w in ORDER.split()]
    return [s for s in steps if (ffn if s[0] in "WMRGUY" else not (first and s[1] < 0) and (following or s[1] < TILES))]


def closing_steps():
    out = [("V", -1, 3), ("A", -1, 2), ("X", -1, 0), ("A", -1, 3), ("O", -1, 1), ("X", -1, 1)]
    return out + FFN_ORDER


FFN_ORDER = [("W", 0, 0), ("W", 0, 1), ("M", 0, 0), ("R", 0, 0)] + [(k, 0, c) for c in range(HC) for k in "GU"] + [("Y", 0, 0), ("Y", 0, 1)]
RINGS = {"P": "pj", "W": "pj", "M": "pj", "R": "pj", "G": "pj", "U": "pj", "Y": "pj", "T": "tr", "V": "tr", "X": "tr", "S": "sc"}
SIZE = {"pj": 3, "tr": 2, "sc": 2}
PRELUDE = [("P", 0, c) for c in range(6)] + [("N", 0, g) for g in range(2)] + [("T", 0, g) for g in range(4)]


def ring_plan(steps, before, shift, taken):
    plan = {}
    for ring, size in SIZE.items():
        uses = [(s, 0) for s in steps if RINGS.get(s[0]) == ring]
        past = [(s, -shift) for s in before if RINGS.get(s[0]) == ring][-size:]
        both = past + uses
        for n, (s, _) in enumerate(uses):
            old = n + len(past) - size
            plan[s] = ((n + taken[ring]) % size, both[old] if old >= 0 else None)
    return plan


def stack(nc, a, sig, v):
    x, pj, tr, av, sc = v.x, v.pj, v.tr, v.av, v.sc
    DONE = B * 2
    xs_ready, xs_high = sig("xs_ready", 4), sig("xs_high")
    pj_full = sig("pj_full", 6, credit=12)
    sq_ready = sig("sq_ready", 4)
    raw_ready = sig("raw_ready", 4)
    cos_ready = sig("cos_ready", 4, credit=2)
    rot_ready = sig("rot_ready", 4)
    ss_ready = sig("ss_ready", 4, credit=2)
    clamped, ln_ready = sig("clamped", 2), sig("ln_ready", 2, credit=2)
    rn_ready = sig("rn_ready", 4)
    sum_ready = sig("sum_ready", 4, credit=2)
    kn_ready = sig("kn_ready", 2)
    qk_full = sig("qk_full", 4, credit=4)
    qk_ready = sig("qk_ready", 4)
    v_ready = sig("v_ready", 2)
    s_full = sig("s_full", 4, credit=4)
    mx_ready = sig("mx_ready", 4)
    nb_ready = sig("nb_ready", 4)
    p_ready = sig("p_ready", 4, credit=8)
    pT_full = sig("pT_full", 4, credit=2)
    pT_ready = sig("pT_ready", 4)
    av_full = sig("av_full", 4, credit=8)
    rs_ready = sig("rs_ready", 2)
    on_ready = sig("on_ready", 2, credit=2)
    oT_full = sig("oT_full", 2, credit=2)
    oT_ready = sig("oT_ready", 2)
    kept = sig("kept")
    table_ready = sig("table_ready", 1)
    f_full = sig("f_full", 6 + 2 * HC, credit=18)
    xa_ready = sig("xa_ready", 2)
    xc_ready = sig("xc_ready", 2)
    sqf_ready = sig("sqf_ready", 1)
    std_ready = sig("std_ready", 1)
    rstd_ready = sig("rstd_ready", 1)
    xm_ready = sig("xm_ready", 1)
    xn_ready = sig("xn_ready", 2)
    gate_ready = sig("gate_ready", HC)
    hid_ready = sig("hid_ready", HC, credit=2)
    x_ready = sig("x_ready", 2, credit=DONE)
    wqkv_loaded = [sig("wqkv_loaded%d" % c, 16, credit=16) for c in range(CHUNKS)]
    scale_loaded = sig("scale_loaded", 16, credit=16)
    ffn_loaded = sig("ffn_loaded", FFN_LOADS * 16)

    def f_count(step):
        return FFN_ORDER.index(step) + 1

    def freed(step):
        kind, t, c = step
        if kind == "P":
            return (raw_ready, c + 1) if c < 4 else (v_ready, c - 3)
        return {"T": (qk_ready, c + 1), "V": (pT_ready, c + 1), "X": (oT_ready, c + 1), "S": (p_ready, c + 1),
                "W": (xa_ready, c + 1), "M": (xc_ready, 2), "R": (std_ready, 1), "G": (gate_ready, c + 1),
                "U": (hid_ready, c + 1), "Y": (x_ready, c + 1)}[kind]

    def bank_free(i, past):
        old, back = past
        signal, n = freed(old)
        return signal.sem, signal.at(unit(i, old, back), n)

    def unit(i, step, back=0):
        if step[0] in "WMRGUY":
            return i - 1 + back
        return (i + back) * TILES + step[1]

    opening = steps_of(True, False, True)
    body = steps_of(False, True, True)
    last = steps_of(False, True, False)
    phases = []
    taken = dict.fromkeys(SIZE, 0)
    before = []
    for begin, count, steps, shift in ((0, 1, PRELUDE, 0), (0, 1, opening, 0), (1, 1, body, 1), (2, ITERS - 3, body, 1),
                                       (ITERS - 1, 1, last, 1), (ITERS, 1, closing_steps(), 1)):
        phases.append((begin, count, steps, ring_plan(steps, before, shift, taken)))
        for ring in SIZE:
            used = sum(RINGS.get(kind) == ring for kind, _, _ in steps)
            assert count == 1 or used % SIZE[ring] == 0
            taken[ring] += used * count
        before = steps

    def run(eng, engine, do):
        def emit(i, steps, plan):
            for step in steps:
                slot, past = plan.get(step, (None, None))
                do(i, step, slot, past)
        for first, count, steps, plan in phases:
            if count == 1:
                emit(first, steps, plan)
            else:
                with eng.Fori(first, first + count) as i:
                    emit(i, steps, plan)

    def head(c, n):
        return 8 * (c // 2) + 2 * n + c % 2

    def row(i, step):
        return (i + step[1] // TILES) % B if step[0] not in "WMRGUY" else (i - 1) % B

    def layer(i, step):
        return (i + step[1] // TILES) // B if step[0] not in "WMRGUY" else (i - 1) // B

    def xrow(k, b, lo=1):
        return x[:, k, bass.ds(b, 1), lo:lo + S].rearrange("p b s -> p (b s)")

    with nc.Block() as block:
        @block.sync
        def _(sp):
            def load_ffn(l):
                def src(name):
                    return a[name][bass.ds(l, 1)]
                sp.dma_start(v.wo[:], src("Wo").rearrange("l (c p) n -> p (l c) n", p=P)).then_inc(ffn_loaded.sem, 16)
                for k in range(KC):
                    sp.dma_start(v.w1[:, k, :], src("W1")[:, k * P:(k + 1) * P, :].rearrange("l p n -> p (l n)")).then_inc(ffn_loaded.sem, 16)
                sp.dma_start(v.w2[:, 0:HC - 1, :], src("W2")[:, 0:(HC - 1) * P, :].rearrange("l (c p) n -> p (l c) n", p=P)).then_inc(ffn_loaded.sem, 16)
                sp.dma_start(v.w2[0:LAST, HC - 1, :], src("W2")[:, (HC - 1) * P:HID, :].rearrange("l p n -> p (l n)")).then_inc(ffn_loaded.sem, 16)
                sp.dma_start(v.small[:], src("small").rearrange("l p n -> p (l n)")).then_inc(ffn_loaded.sem, 16)

            def load_chunk(l, c):
                sp.dma_start(v.wqkv[:, c].rearrange("p a k n -> p (a k n)").bitcast(F32),
                             a["parts"][bass.ds(l, 1), c].rearrange("l p n -> p (l n)")).then_inc(wqkv_loaded[c].sem, 16)

            def load_scale(l):
                sp.dma_start(v.qk_scale[:], a["qk_scale"][bass.ds(l, 1), :].rearrange("l n -> (l n)").partition_broadcast(P)).then_inc(scale_loaded.sem, 16)
            for c in range(CHUNKS):
                sp.drain().then_inc(wqkv_loaded[c].sem, wqkv_loaded[c].credit)
            sp.drain().then_inc(scale_loaded.sem, scale_loaded.credit)
            load_ffn(0)
            with sp.Fori(1, DEPTH) as l:
                sp.wait_ge(table_ready.sem, table_ready.at(l * B, 0))
                load_scale(l)
                for c in range(CHUNKS):
                    sp.wait_ge(pj_full.sem, pj_full.at(l * (B * TILES) - 1, c + 1))
                    load_chunk(l, c)
                sp.wait_ge(x_ready.sem, x_ready.at(l * B, 0))
                load_ffn(l)
            sp.wait_ge(f_full.sem, f_full.at(ITERS - 1, 2))
            for k in range(KC):
                sp.dma_start(v.kept[k], a["kept"][:, k, :, :]).then_inc(kept.sem, 16)
            sp.wait_ge(kept.sem, 16 * KC)

        @block.gpsimd
        def _(pool):
            pool.drain().then_inc(sum_ready.sem, sum_ready.credit)
            pool.drain().then_inc(cos_ready.sem, cos_ready.credit)
            def do(i, step, slot, past):
                kind, t, c = step
                if kind == "P":
                    tau = unit(i, step)
                    if c == 0:
                        b = row(i, step)
                        pool.wait_ge(x_ready.sem, x_ready.at(i + t // TILES - B, 2))
                        pool.wait_ge(pj_full.sem, pj_full.at(tau - 2, 6))
                        def cols(k):
                            lo = 1 - k + (t % TILES) * P
                            return x[:, k, bass.ds(b, 1), lo:lo + P].rearrange("p b s -> p (b s)")
                        for k in range(KC):
                            pool.tensor_copy(v.xs[:, t % 2, 0, k, :], cols(k)).then_inc(xs_ready.sem, 1)
                        pool.wait_ge(xs_ready.sem, xs_ready.at(tau, KC))
                        pool.nop().then_inc(xs_high.sem, 1)
                        for k in range(KC):
                            pool.tensor_tensor(v.xs[:, t % 2, 1, k, :], cols(k), v.xs[:, t % 2, 0, k, :], ALU.subtract).then_inc(xs_ready.sem, 1)
                    if c < 4:
                        pool.wait_ge(raw_ready.sem, raw_ready.at(tau, c + 1))
                        pool.wait_ge(qk_full.sem, qk_full.at(tau - 1, c + 1))
                        base = 2 * DH * (c % 2)
                        cos = v.table[:, t % TILES:t % TILES + 1, base:base + DH]
                        q3 = v.qk[:, c, :].rearrange("p (h d) -> p h d", h=8)
                        if c == 0 and t % TILES == 0:
                            pool.wait_ge(table_ready.sem, table_ready.at(i + t // TILES, 1))
                        pool.tensor_tensor(q3, v.raw[:, c % 2, :].rearrange("p (h d) -> p h d", h=8), bcast(cos, (P, 8, DH)),
                                           ALU.mult).then_inc(cos_ready.sem, 1)
                        pool.wait_ge(cos_ready.sem, cos_ready.at(tau, c + 1))
                        pool.wait_ge(rot_ready.sem, rot_ready.at(tau, c + 1))
                        pool.tensor_tensor(v.qk[:, c, :], v.qk[:, c, :], v.rot_b[:, c % 2, :], ALU.add).then_inc(sum_ready.sem, 1)
                if kind == "N":
                    tau = unit(i, step)
                    pool.wait_ge(rn_ready.sem, rn_ready.at(tau, 2 * c + 1))
                    pool.wait_ge(sum_ready.sem, sum_ready.at(tau, 2 * c + 2))
                    k3 = v.qk[:, 2 * c + 1, :].rearrange("p (h d) -> p h d", h=8)
                    r3 = v.rn[:, t % 2, 16 * c + 8:16 * c + 16].unsqueeze(2)
                    pool.tensor_tensor(k3, k3, bcast(r3, (P, 8, DH)), ALU.mult).then_inc(kn_ready.sem, 1)
            run(pool, "pool", do)

        @block.tensor
        def _(pe):
            pe.drain().then_inc(pj_full.sem, pj_full.credit)
            pe.drain().then_inc(qk_full.sem, qk_full.credit)
            pe.drain().then_inc(av_full.sem, av_full.credit)
            pe.drain().then_inc(s_full.sem, s_full.credit)
            pe.drain().then_inc(pT_full.sem, pT_full.credit)
            pe.drain().then_inc(f_full.sem, f_full.credit)
            pe.drain().then_inc(oT_full.sem, oT_full.credit)
            def do(i, step, slot, past):
                kind, t, c = step
                u = unit(i, step)
                ts = t % TILES
                if kind == "P":
                    if c == 0:
                        pe.wait_ge(xs_ready.sem, xs_ready.at(u, 4))
                    if ts == 0:
                        pe.wait_ge(wqkv_loaded[c].sem, wqkv_loaded[c].at(layer(i, step), 0))
                    if past:
                        pe.wait_ge(*bank_free(i, past))
                    products = [(0, 0), (0, 1), (1, 0)]
                    for n, (xp, wp) in enumerate(products):
                        for k in range(KC):
                            mm = pe.matmul(pj[slot][:], v.xs[:, t % 2, xp, k, :], v.wqkv[:, c, wp, k, :],
                                           start=(n == 0 and k == 0), stop=(n == 2 and k == KC - 1))
                    mm.then_inc(pj_full.sem, 1)
                if kind == "T":
                    if c % 2 == 0:
                        pe.wait_ge(sum_ready.sem, sum_ready.at(u, c + 1))
                    else:
                        pe.wait_ge(kn_ready.sem, kn_ready.at(u, c // 2 + 1))
                    if past:
                        pe.wait_ge(*bank_free(i, past))
                    for n in range(4):
                        mm = pe.transpose(tr[slot][:, n * P:(n + 1) * P], v.qk[:, c, n * P:(n + 1) * P], v.ident[:])
                    mm.then_inc(qk_full.sem, 1)
                if kind == "S":
                    pe.wait_ge(qk_ready.sem, qk_ready.at(u, 2 * (c // 2) + 2))
                    if past:
                        pe.wait_ge(*bank_free(i, past))
                    out = sc[:, slot, :]
                    first = ts == 0
                    pe.matmul(out, v.ident16[:], bcast(v.mask16[:, 0:1, :] if first else v.mask16[:, 1:2, :], (P, 4, P)),
                              start=True, stop=False, skip_group_check=True)
                    for n in range(4):
                        h = head(c, n)
                        r = slice(DH * (h % 2), DH * (h % 2) + DH)
                        q, kc, kp = v.qT[r, h // 2, :], v.kT[r, t % 2, h // 2, :], v.kT[r, 1 - t % 2, h // 2, :]
                        o = n * P
                        if not first:
                            pe.matmul(sc[0:W, slot, o + W:o + P], q[:, 0:W], kp[:, W:P], start=False, stop=False, skip_group_check=True)
                        pe.matmul(sc[0:W, slot, o:o + W], q[:, 0:W], kc[:, 0:W], start=False, stop=False, skip_group_check=True)
                        mm = pe.matmul(sc[W:P, slot, o:o + P], q[:, W:P], kc, start=False, stop=(n == 3), skip_group_check=True)
                    mm.then_inc(s_full.sem, 1)
                if kind == "V":
                    pe.wait_ge(p_ready.sem, p_ready.at(u, c + 1))
                    if past:
                        pe.wait_ge(*bank_free(i, past))
                    for n in range(4):
                        mm = pe.transpose(tr[slot][:, n * P:(n + 1) * P], v.probs[:, c % 2, n * P:(n + 1) * P], v.ident[:])
                    mm.then_inc(pT_full.sem, 1)
                if kind == "A":
                    pe.wait_ge(pT_ready.sem, pT_ready.at(u, c + 1))
                    pe.wait_ge(v_ready.sem, v_ready.at(u, c // 2 + 1))
                    if c % 2 == 0:
                        pe.wait_ge(on_ready.sem, on_ready.at(u, c // 2))
                    for n in range(4):
                        h = head(c, n)
                        o = (h % 8) * DH
                        pe.matmul(av[0:W, o:o + DH], v.pT[:, c % 2, n * P:n * P + W], v.v_even[:, ts, h * DH:(h + 1) * DH], start=True, stop=True)
                        mm = pe.matmul(av[W:P, o:o + DH], v.pT[:, c % 2, n * P + W:(n + 1) * P], v.v_odd[:, t % 2, h * DH:(h + 1) * DH], start=True, stop=True)
                    mm.then_inc(av_full.sem, 1)
                if kind == "X":
                    pe.wait_ge(on_ready.sem, on_ready.at(u, c + 1))
                    if past:
                        pe.wait_ge(*bank_free(i, past))
                    for n in range(4):
                        mm = pe.transpose(tr[slot][:, n * P:(n + 1) * P], v.on[:, c, n * P:(n + 1) * P], v.ident[:])
                    mm.then_inc(oT_full.sem, 1)
                if kind == "W":
                    if c == 0:
                        pe.wait_ge(oT_ready.sem, oT_ready.at((u + 1) * TILES, 0))
                        pe.wait_ge(ffn_loaded.sem, ffn_loaded.at(layer(i, step), FFN_LOADS * 16))
                    if past:
                        pe.wait_ge(*bank_free(i, past))
                    for n in range(PAIRS):
                        mm = pe.matmul(pj[slot][:], v.wo[:, n, c * P:(c + 1) * P], v.oT[:, n, :], start=(n == 0), stop=(n == PAIRS - 1))
                if kind == "M":
                    pe.wait_ge(xa_ready.sem, xa_ready.at(u, 2))
                    if past:
                        pe.wait_ge(*bank_free(i, past))
                    for k in range(KC):
                        mm = pe.matmul(pj[slot][:], v.mean_w[:], xrow(k, row(i, step), 1 - k), start=(k == 0), stop=(k == KC - 1))
                if kind == "R":
                    pe.wait_ge(sqf_ready.sem, sqf_ready.at(u, 1))
                    if past:
                        pe.wait_ge(*bank_free(i, past))
                    for k in range(KC):
                        mm = pe.matmul(pj[slot][:], v.mean_w[:], v.sqf[:, k, :], start=(k == 0), stop=(k == KC - 1))
                if kind in "GU":
                    n = P if c < HC - 1 else LAST
                    col = c * P + (HID if kind == "G" else 0)
                    if kind == "G" and c == 0:
                        pe.wait_ge(xn_ready.sem, xn_ready.at(u, 2))
                    if past:
                        pe.wait_ge(*bank_free(i, past))
                    for k in range(KC):
                        mm = pe.matmul(pj[slot][0:n, :], v.w1[:, k, col:col + n], v.xc[:, k, :], start=(k == 0), stop=(k == KC - 1))
                if kind == "Y":
                    pe.wait_ge(hid_ready.sem, hid_ready.at(u, HC))
                    if past:
                        pe.wait_ge(*bank_free(i, past))
                    for n in range(HC):
                        r = P if n < HC - 1 else LAST
                        mm = pe.matmul(pj[slot][:], v.w2[0:r, n, c * P:(c + 1) * P], v.hid[0:r, n, :], start=(n == 0), stop=(n == HC - 1))
                if kind in "WMRGUY":
                    mm.then_inc(f_full.sem, 1)
            run(pe, "pe", do)

        @block.scalar
        def _(act):
            act.drain().then_inc(p_ready.sem, p_ready.credit)
            act.drain().then_inc(ln_ready.sem, ln_ready.credit)
            act.preload_act_table_set(EXP_AND_LN)
            def do(i, step, slot, past):
                kind, t, c = step
                u = unit(i, step)
                ts = t % TILES
                if kind == "P":
                    act.wait_ge(pj_full.sem, pj_full.at(u, c + 1))
                if kind == "P" and c < 4:
                    act.wait_ge(ss_ready.sem, ss_ready.at(u, c - 1))
                    act.wait_ge(cos_ready.sem, cos_ready.at(u, c - 1))
                    act.activation(v.raw[:, c % 2, :], pj[slot][:], ACT.Copy).then_inc(raw_ready.sem, 1)
                    act.wait_ge(raw_ready.sem, raw_ready.at(u, c + 1))
                    act.wait_ge(ss_ready.sem, ss_ready.at(u, c))
                    act.activation(v.sq[:], v.raw[:, c % 2, :], ACT.Square).then_inc(sq_ready.sem, 1)
                if kind == "P" and c >= 4:
                    cs = slice((c - 4) * 512, (c - 3) * 512)
                    act.wait_ge(av_full.sem, av_full.at(u - 2, 4))
                    act.activation(v.v_odd[:, t % 2, cs], pj[slot][:], ACT.Copy)
                    if ts < TILES - 1:
                        act.activation(v.v_even[W:P, ts + 1, cs], pj[slot][W:P, :], ACT.Copy)
                    act.activation(v.v_even[0:W, ts, cs], pj[slot][0:W, :], ACT.Copy).then_inc(v_ready.sem, 1)
                if kind == "N":
                    own = slice(16 * c, 16 * c + 16)
                    act.wait_ge(clamped.sem, clamped.at(u, c + 1))
                    act.activation(v.ln_ss[:, own], v.ss[:, own], ACT.Ln).then_inc(ln_ready.sem, 1)
                    act.wait_ge(ln_ready.sem, ln_ready.at(u, c + 1))
                    act.wait_ge(p_ready.sem, p_ready.at(u - 2, 4))
                    ln, rn = v.ln_ss[:, own], v.rn[:, t % 2, own]
                    act.activation(rn[:, 8:16], ln[:, 8:16], ACT.Exp, scale=-0.5).then_inc(rn_ready.sem, 1)
                    act.activation(rn[:, 0:8], ln[:, 0:8], ACT.Exp, bias=v.ln8[:], scale=-0.5).then_inc(rn_ready.sem, 1)
                if kind == "T":
                    act.wait_ge(qk_full.sem, qk_full.at(u, c + 1))
                    act.wait_ge(s_full.sem, s_full.at(u - 1, 2 * (c // 2) + 2))
                    hp = slice(4 * (c // 2), 4 * (c // 2) + 4)
                    dst = v.qT[:, hp, :] if c % 2 == 0 else v.kT[:, t % 2, hp, :]
                    act.activation(dst, tr[slot][:].rearrange("p (n q) -> p n q", n=4), ACT.Copy).then_inc(qk_ready.sem, 1)
                if kind == "S":
                    act.wait_ge(nb_ready.sem, nb_ready.at(u, c + 1))
                    act.wait_ge(pT_full.sem, pT_full.at(u, c - 1))
                    for n in range(4):
                        h = head(c, n)
                        col = 16 * (h // 8) + h % 8
                        e = act.activation(v.probs[:, c % 2, n * P:(n + 1) * P], sc[:, slot, n * P:(n + 1) * P], ACT.Exp,
                                           bias=v.nb[:, c % 2, n:n + 1], scale=v.rn[:, t % 2, col:col + 1],
                                           accum_out=v.psums[:, t % 2, h:h + 1])
                    e.then_inc(p_ready.sem, 1)
                if kind == "X":
                    act.wait_ge(oT_full.sem, oT_full.at(u, c + 1))
                    if ts == 0 and c == 0:
                        act.wait_ge(f_full.sem, f_full.at(i - 1, 2))
                    act.activation(v.oT[:, 4 * c:4 * c + 4, ts * P:(ts + 1) * P], tr[slot][:].rearrange("p (n q) -> p n q", n=4),
                                   ACT.Copy).then_inc(oT_ready.sem, 1)
                if kind == "R":
                    act.wait_ge(f_full.sem, f_full.at(u, f_count(step)))
                    act.activation(v.std, pj[slot][:], ACT.Ln, bias=v.eps[:]).then_inc(std_ready.sem, 1)
                    act.wait_ge(std_ready.sem, std_ready.at(u, 1))
                    act.activation(v.std, v.std, ACT.Exp, scale=-0.5).then_inc(rstd_ready.sem, 1)
                if kind == "M":
                    act.wait_ge(xc_ready.sem, xc_ready.at(u, 2))
                    act.activation(v.sqf, v.xc[:], ACT.Square).then_inc(sqf_ready.sem, 1)
                if kind == "G":
                    n = P if c < HC - 1 else LAST
                    act.wait_ge(f_full.sem, f_full.at(u, f_count(step)))
                    act.wait_ge(hid_ready.sem, hid_ready.at(u, c - 1))
                    act.activation(v.gate[0:n, c % 2, :], pj[slot][0:n, :], ACT.Gelu, bias=v.b1c[0:n, HC + c:HC + c + 1]).then_inc(gate_ready.sem, 1)
                    if c == HC - 1:
                        act.preload_act_table_set(EXP_AND_LN)
            run(act, "act", do)

        @block.vector
        def _(dve):
            dve.drain().then_inc(x_ready.sem, x_ready.credit)
            dve.drain().then_inc(hid_ready.sem, hid_ready.credit)
            dve.drain().then_inc(ss_ready.sem, ss_ready.credit)
            dve.drain().then_inc(on_ready.sem, on_ready.credit)

            def do(i, step, slot, past):
                kind, t, c = step
                u = unit(i, step)
                ts = t % TILES
                if kind == "P" and c == 0 and ts == 0:
                    pair = i + t // TILES
                    dve.wait_ge(scale_loaded.sem, scale_loaded.at(layer(i, step), 0))
                    dve.tensor_tensor(v.table[:], v.rotary[:], bcast(v.qk_scale[:].unsqueeze(1), (P, TILES, 4 * DH)), ALU.mult).then_inc(table_ready.sem, 1)
                    dve.wait_ge(table_ready.sem, table_ready.at(pair, 1))
                if kind == "P" and c < 4:
                    dve.wait_ge(raw_ready.sem, raw_ready.at(u, c + 1))
                    dve.wait_ge(sum_ready.sem, sum_ready.at(u, c - 1))
                    src = v.raw[:, c % 2, :].rearrange("p (h d) -> p h d", h=8)
                    base = 2 * DH * (c % 2)
                    sin = v.table[:, ts:ts + 1, base + DH:base + 2 * DH]
                    dst_b = v.rot_b[:, c % 2, :].rearrange("p (h d) -> p h d", h=8)
                    hf = DH // 2
                    dve.tensor_tensor(dst_b[:, :, 0:hf], src[:, :, hf:DH], bcast(sin[:, :, 0:hf], (P, 8, hf)), ALU.mult)
                    dve.tensor_tensor(dst_b[:, :, hf:DH], src[:, :, 0:hf], bcast(sin[:, :, hf:DH], (P, 8, hf)), ALU.mult).then_inc(rot_ready.sem, 1)
                    dve.wait_ge(sq_ready.sem, sq_ready.at(u, c + 1))
                    if c % 2 == 0:
                        dve.wait_ge(ln_ready.sem, ln_ready.at(u - 1, c // 2 + 1))
                    dve.tensor_reduce(v.ss[:, 8 * c:8 * c + 8], v.sq[:].rearrange("p (h d) -> p h d", h=8), AX.X, ALU.add).then_inc(ss_ready.sem, 1)
                if kind == "N":
                    dve.wait_ge(ss_ready.sem, ss_ready.at(u, 2 * c + 2))
                    ss = v.ss[:, 16 * c:16 * c + 16]
                    dve.tensor_scalar(ss, ss, 1e-24, None, ALU.max).then_inc(clamped.sem, 1)
                if kind == "S":
                    dve.wait_ge(s_full.sem, s_full.at(u, c + 1))
                    dve.wait_ge(rn_ready.sem, rn_ready.at(u, 2 * (c // 2) + 2))
                    own = slice(16 * (c // 2) + c % 2, 16 * (c // 2) + 8, 2)
                    dve.tensor_reduce(v.mx[:, c % 2, :], sc[:, slot, :].rearrange("p (h j) -> p h j", h=4), AX.X, ALU.max).then_inc(mx_ready.sem, 1)
                    dve.wait_ge(mx_ready.sem, mx_ready.at(u, c + 1))
                    dve.wait_ge(p_ready.sem, p_ready.at(u, c - 1))
                    dve.scalar_tensor_tensor(v.nb[:, c % 2, :], v.mx[:, c % 2, :], -1.0, v.rn[:, t % 2, own], ALU.mult, ALU.mult).then_inc(nb_ready.sem, 1)
                if kind == "V":
                    dve.wait_ge(pT_full.sem, pT_full.at(u, c + 1))
                    dve.wait_ge(av_full.sem, av_full.at(u, c - 1))
                    dve.tensor_copy(v.pT[:, c % 2, :], tr[slot][:]).then_inc(pT_ready.sem, 1)
                if kind == "O":
                    dve.wait_ge(p_ready.sem, p_ready.at(u, 2 * c + 2))
                    dve.reciprocal(v.rs[:, c, :], v.psums[:, t % 2, 8 * c:8 * c + 8]).then_inc(rs_ready.sem, 1)
                    dve.wait_ge(rs_ready.sem, rs_ready.at(u, c + 1))
                    dve.wait_ge(av_full.sem, av_full.at(u, 2 * c + 2))
                    dve.wait_ge(oT_full.sem, oT_full.at(u - 1, c + 1))
                    dve.tensor_tensor(v.on[:, c, :].rearrange("p (h d) -> p h d", h=8), av[:].rearrange("p (h d) -> p h d", h=8),
                                      bcast(v.rs[:, c, :].unsqueeze(2), (P, 8, DH)), ALU.mult).then_inc(on_ready.sem, 1)
                if kind == "W":
                    dve.wait_ge(f_full.sem, f_full.at(u, f_count(step)))
                    xr = xrow(c, row(i, step))
                    dve.tensor_tensor(xr, xr, pj[slot][:], ALU.add).then_inc(xa_ready.sem, 1)
                if kind == "M":
                    dve.wait_ge(f_full.sem, f_full.at(u, f_count(step)))
                    dve.wait_ge(xa_ready.sem, xa_ready.at(u, 2))
                    for k in range(KC):
                        dve.tensor_tensor(v.xc[:, k, :], xrow(k, row(i, step), 1 - k), pj[slot][:], ALU.subtract).then_inc(xc_ready.sem, 1)
                if kind == "R":
                    dve.wait_ge(rstd_ready.sem, rstd_ready.at(u, 1))
                    dve.tensor_tensor(v.xc[:], v.xc[:], bcast(v.std.unsqueeze(1), (P, KC, S)), ALU.mult).then_inc(xm_ready.sem, 1)
                    dve.wait_ge(xm_ready.sem, xm_ready.at(u, 1))
                    for k in range(KC):
                        dve.tensor_scalar(v.xc[:, k, :], v.xc[:, k, :], v.lng[:, k:k + 1], v.lnb[:, k:k + 1], ALU.mult, ALU.add).then_inc(xn_ready.sem, 1)
                if kind == "U":
                    n = P if c < HC - 1 else LAST
                    dve.wait_ge(f_full.sem, f_full.at(u, f_count(step)))
                    dve.wait_ge(gate_ready.sem, gate_ready.at(u, c + 1))
                    dve.scalar_tensor_tensor(v.hid[0:n, c, :], pj[slot][0:n, :], v.b1c[0:n, c:c + 1], v.gate[0:n, c % 2, :],
                                             ALU.add, ALU.mult).then_inc(hid_ready.sem, 1)
                if kind == "Y":
                    dve.wait_ge(f_full.sem, f_full.at(u, f_count(step)))
                    xr = xrow(c, row(i, step))
                    dve.scalar_tensor_tensor(xr, pj[slot][:], v.b2c[:, c:c + 1], xr, ALU.add, ALU.add).then_inc(x_ready.sem, 1)
            run(dve, "dve", do)


def final(nc, a, sig, v):
    summed, stored = sig("z_sum"), sig("z_stored")
    with nc.Block() as block:
        @block.sync
        def _(sp):
            for k in range(KC):
                sp.wait_ge(summed.sem, k + 1)
                sp.dma_start(a["out"][:, k, :, :], v.kept[k]).then_inc(stored.sem, 16)
            sp.wait_ge(stored.sem, 16 * KC)

        @block.vector
        def _(dve):
            for k in range(KC):
                dve.scalar_tensor_tensor(v.kept[k], v.x[:, k, :, 1:ROW], v.tanhs[:, 1:2], v.kept[k], ALU.mult, ALU.add).then_inc(summed.sem, 1)


def constants():
    f = np.float32
    half = np.arange(0, DH, 2, dtype=f)
    inv_freq = (f(1.0) / f(10000.0) ** (half / f(DH))).astype(f)
    tok = np.arange(S, dtype=f)
    freqs = tok[:, None] * inv_freq[None, :]
    base = ((half + f(0.4 * DH)) / f(1.4 * DH)).astype(f)
    power = ((tok - S // 2) / (W // 2)).astype(f)
    scale = base[None, :] ** power[:, None]
    cos, sin = np.cos(freqs), np.sin(freqs)
    inv = f(1.0) / scale
    rot = np.concatenate([cos * scale, cos * scale, -sin * scale, sin * scale,
                          cos * inv, cos * inv, -sin * inv, sin * inv], -1).astype(f)
    rotary = np.ascontiguousarray(rot.reshape(TILES, P, 4 * DH).transpose(1, 0, 2))
    mask = np.zeros((P, 2, P), f)
    i = np.arange(W)[:, None]
    j = np.arange(W)[None, :]
    causal, band = np.where(j <= i, 0.0, MASKED), np.where(j >= i, 0.0, MASKED)
    for first in range(2):
        mask[0:W, first, 0:W] = causal
        mask[0:W, first, W:P] = MASKED if first == 0 else band
        mask[W:P, first, 0:W] = band
        mask[W:P, first, W:P] = causal
    block = np.zeros((P, 8), f)
    block[np.arange(P), np.arange(P) // XD] = 1.0
    return {"rotary": rotary, "mask": mask, "bmask": block, "ident": np.eye(P, dtype=f),
            "mean_w": np.full((P, P), 1.0 / D, f)}


def lay_out(inp):
    g = {k: np.asarray(x) for k, x in inp.items()}

    def chunks(m):
        return np.ascontiguousarray(m.reshape(KC, P, -1).transpose(1, 0, 2))

    def column(x):
        return x.reshape(KC, P).T
    out = dict(constants())
    out["xT"] = chunks(g["x"].transpose(2, 0, 1).reshape(D, B * S)).reshape(P, KC, B, S)
    out["ctxT"] = chunks(g["ctx_1024"].transpose(2, 0, 1).reshape(D, B * CTX)).reshape(P, KC, B, CTX)
    out["g_xattn"], out["g_ffn"] = g["g_xattn"].reshape(1), g["g_ffn"].reshape(1)
    for name, w in (("Wq", "Wq"), ("Wk", "Wk"), ("Wv", "Wv"), ("Wo_x", "Wo")):
        out[name] = chunks(g["L0_xattn_" + w].T)
    out["cols"] = np.ascontiguousarray(np.concatenate([column(g["L0_xattn_" + n]) for n in ("bq", "bk", "bo")], 1))
    out["bv"] = g["L0_xattn_bv"]
    out["mlp"] = np.ascontiguousarray(np.concatenate([g["L0_xattn_w1"], g["L0_xattn_b1"][:, None], g["L0_xattn_w2"].T, np.zeros((CTX, P - CTX), np.float32), g["L0_xattn_b2"][:, None]], 1))
    out["w3"], out["b3"] = np.ascontiguousarray(g["L0_xattn_w3"].T), g["L0_xattn_b3"]
    qs, ks = g["L0_ffn_q_scale"], g["L0_ffn_k_scale"]
    swap = lambda s: np.concatenate([s[:, DH // 2:], s[:, :DH // 2]], 1)
    out["qk_scale"] = np.ascontiguousarray(np.concatenate([qs, swap(qs), ks, swap(ks)], 1))
    out["Wqkv"], out["Wo"], out["W1"], out["W2"] = (g["L0_ffn_" + n] for n in ("Wqkv", "Wo", "W1", "W2"))
    b1 = np.zeros((DEPTH, 2, HC * P), np.float32)
    b1[:, :, :HID] = g["L0_ffn_b1"].reshape(DEPTH, 2, HID)
    b1 = b1.reshape(DEPTH, 2 * HC, P).transpose(0, 2, 1)
    rest = [g["L0_ffn_" + n].reshape(DEPTH, KC, P).transpose(0, 2, 1) for n in ("b2", "ln_g", "ln_b")]
    out["small"] = np.ascontiguousarray(np.concatenate([b1] + rest, 2))
    return out


def kernel(**inputs):
    import concourse.bacc as bacc
    from concourse.bass_utils import run_bass_kernel_spmd

    nc = bacc.Bacc("TRN2", target_bir_lowering=False, num_devices=1)
    arrays = lay_out(inputs)
    a = {n: nc.dram_tensor("in_" + n, x.shape, F32, kind="ExternalInput").ap() for n, x in arrays.items()}
    a["kept"] = nc.dram_tensor("kept", (P, KC, B, S), F32, kind="Internal").ap()
    a["parts"] = nc.dram_tensor("parts", (DEPTH, CHUNKS, P, 2 * KC * 512), F32, kind="Internal").ap()
    a["out"] = nc.dram_tensor("out_stream", (P, KC, B, S), F32, kind="ExternalOutput").ap()
    build(nc, a)
    r = run_bass_kernel_spmd(nc, [{"in_" + n: np.ascontiguousarray(x) for n, x in arrays.items()}], core_ids=[0])
    y = r.results[0]["out_stream"]
    return np.ascontiguousarray(y.transpose(2, 3, 1, 0).reshape(B, S, D))
```
